# Optimizing a Trainium2 kernel written in Bass

```python
import numpy as np
import jax
import jax.numpy as jnp

def _softmax(x, axis=-1):
    return jax.nn.softmax(x, axis=axis)

def _gelu(x):
    return jax.nn.gelu(x, approximate=True)

def _silu(x):
    return jax.nn.silu(x)

def _sigmoid(x):
    return jax.nn.sigmoid(x)

def _layernorm(x, axis=-1, eps=1e-05):
    m = jnp.mean(x, axis=axis, keepdims=True)
    v = jnp.var(x, axis=axis, keepdims=True)
    return (x - m) / jnp.sqrt(v + eps)

def _scatter_add(tgt, idx, src, axis=0):
    return tgt.at[idx].add(src)

def _segment_sum(src, seg, n):
    return jax.ops.segment_sum(src, seg, n)
kernel_name = 'mk_sandwich_d1_jaxref_r8_128839'

def setup_inputs(seed: int=0):
    np.random.seed(seed)
    _w = jnp.asarray

    def _L0_attn_setup():
        import jax, jax.numpy as jnp
        import numpy as np
        INFTY_APPROX = 1e+30
        ROTARY_BASE = 10000.0
        ATTN_SCALE = 1.0 / 128.0

        def rope(x):
            T, D = (x.shape[-2], x.shape[-1])
            half = D // 2
            pos = jnp.arange(T, dtype=jnp.float32)[:, None]
            freqs = jnp.power(ROTARY_BASE, -jnp.arange(half, dtype=jnp.float32) / half)[None, :]
            rad = pos * freqs
            cos = jnp.cos(rad).astype(x.dtype)
            sin = jnp.sin(rad).astype(x.dtype)
            even, odd = jnp.split(x, 2, axis=-1)
            r_even = even * cos - odd * sin
            r_odd = even * sin + odd * cos
            return jnp.concatenate([r_even, r_odd], axis=-1)
        key = jax.random.key(seed)
        ks = jax.random.split(key, 5)
        B, T, M, H, D = (2, 256, 256, 16, 128)
        stddev = M ** (-0.5)
        return {'x': jax.random.normal(ks[0], (B, T, M), dtype=jnp.float32), 'wq': stddev * jax.random.normal(ks[1], (M, H, D), dtype=jnp.float32), 'wk': stddev * jax.random.normal(ks[2], (M, H, D), dtype=jnp.float32), 'wv': stddev * jax.random.normal(ks[3], (M, H, D), dtype=jnp.float32), 'wo': stddev * jax.random.normal(ks[4], (H, D, M), dtype=jnp.float32)}
    _L0_attn_in = _L0_attn_setup()

    def _L0_ffn_setup():
        import jax, jax.numpy as jnp
        import numpy as np
        ALPHA = 1.702
        LIMIT = 7.0
        TOP_K = 4
        B, S, H = (1, 128, 256)
        E, D = (16, 256)
        key = jax.random.key(seed)
        ks = jax.random.split(key, 7)
        s = 0.02
        return {'hidden_states': jax.random.normal(ks[0], (B, S, H), dtype=jnp.float32), 'router_weight': jax.random.normal(ks[1], (E, H), dtype=jnp.float32) * s, 'router_bias': jax.random.normal(ks[2], (E,), dtype=jnp.float32) * s, 'gate_up_proj': jax.random.normal(ks[3], (E, H, 2 * D), dtype=jnp.float32) * s, 'gate_up_proj_bias': jax.random.normal(ks[4], (E, 2 * D), dtype=jnp.float32) * s, 'down_proj': jax.random.normal(ks[5], (E, D, H), dtype=jnp.float32) * s, 'down_proj_bias': jax.random.normal(ks[6], (E, H), dtype=jnp.float32) * s}
    _L0_ffn_in = _L0_ffn_setup()
    _d = {'L0_attn_x': _L0_attn_in['x'], 'L0_attn_wq': _L0_attn_in['wq'], 'L0_attn_wk': _L0_attn_in['wk'], 'L0_attn_wv': _L0_attn_in['wv'], 'L0_attn_wo': _L0_attn_in['wo'], 'L0_ffn_router_weight': _L0_ffn_in['router_weight'], 'L0_ffn_router_bias': _L0_ffn_in['router_bias'], 'L0_ffn_gate_up_proj': _L0_ffn_in['gate_up_proj'], 'L0_ffn_gate_up_proj_bias': _L0_ffn_in['gate_up_proj_bias'], 'L0_ffn_down_proj': _L0_ffn_in['down_proj'], 'L0_ffn_down_proj_bias': _L0_ffn_in['down_proj_bias']}
    _x0 = _d['L0_attn_x']
    _d['L0_attn_x'] = jax.random.normal(jax.random.fold_in(jax.random.key(seed), 1), (4, 256, 256), dtype=_x0.dtype)
    del _x0
    return _d

def reference(L0_attn_x, L0_attn_wq, L0_attn_wk, L0_attn_wv, L0_attn_wo, L0_ffn_router_weight, L0_ffn_router_bias, L0_ffn_gate_up_proj, L0_ffn_gate_up_proj_bias, L0_ffn_down_proj, L0_ffn_down_proj_bias):

    def _L0_attn_ref(x, wq, wk, wv, wo):
        import jax, jax.numpy as jnp
        import numpy as np
        INFTY_APPROX = 1e+30
        ROTARY_BASE = 10000.0
        ATTN_SCALE = 1.0 / 128.0

        def rope(x):
            T, D = (x.shape[-2], x.shape[-1])
            half = D // 2
            pos = jnp.arange(T, dtype=jnp.float32)[:, None]
            freqs = jnp.power(ROTARY_BASE, -jnp.arange(half, dtype=jnp.float32) / half)[None, :]
            rad = pos * freqs
            cos = jnp.cos(rad).astype(x.dtype)
            sin = jnp.sin(rad).astype(x.dtype)
            even, odd = jnp.split(x, 2, axis=-1)
            r_even = even * cos - odd * sin
            r_odd = even * sin + odd * cos
            return jnp.concatenate([r_even, r_odd], axis=-1)
        T = x.shape[1]
        q = jnp.einsum('bim,mhd->bhid', x, wq)
        k = jnp.einsum('bim,mhd->bhid', x, wk)
        v = jnp.einsum('bim,mhd->bhid', x, wv)
        q = rope(q)
        k = rope(k)
        mult = jnp.asarray(ATTN_SCALE ** 0.5, dtype=x.dtype)
        s = jnp.einsum('bhid,bhjd->bhij', q * mult, k * mult)
        i = jnp.arange(T)[:, None]
        j = jnp.arange(T)[None, :]
        mask = jnp.less(i, j).astype(s.dtype)[None, None, :, :]
        s = s - jnp.asarray(INFTY_APPROX, dtype=s.dtype) * mask
        p = jax.nn.softmax(s, axis=-1)
        o = jnp.einsum('bhij,bhjd->bhid', p, v)
        r = jnp.einsum('bhid,hdm->bim', o, wo)
        return r

    def _L0_ffn_ref(hidden_states, router_weight, router_bias, gate_up_proj, gate_up_proj_bias, down_proj, down_proj_bias):
        import jax, jax.numpy as jnp
        import numpy as np
        ALPHA = 1.702
        LIMIT = 7.0
        TOP_K = 4
        B, S, H = (1, 128, 256)
        E, D = (16, 256)
        batch, seq, hdim = hidden_states.shape
        x = hidden_states.reshape(-1, hdim)
        T = x.shape[0]
        logits = x @ router_weight.T + router_bias
        top_val, top_idx = jax.lax.top_k(logits, TOP_K)
        top_val = jax.nn.softmax(top_val, axis=-1)
        router_scores = jnp.zeros_like(logits).at[jnp.arange(T)[:, None], top_idx].set(top_val)
        gate_up = jnp.einsum('th,ehd->etd', x, gate_up_proj) + gate_up_proj_bias[:, None, :]
        gate = gate_up[..., ::2]
        up = gate_up[..., 1::2]
        gate = jnp.minimum(gate, LIMIT)
        up = jnp.clip(up, -LIMIT, LIMIT)
        glu = gate * jax.nn.sigmoid(gate * ALPHA)
        out = jnp.einsum('etd,edh->eth', (up + 1.0) * glu, down_proj) + down_proj_bias[:, None, :]
        out = out * router_scores.T[:, :, None]
        out = out.sum(axis=0)
        return out.reshape(batch, seq, hdim)
    x = L0_attn_x
    x = x + _layernorm(_L0_attn_ref(_layernorm(x, axis=-1), L0_attn_wq, L0_attn_wk, L0_attn_wv, L0_attn_wo), axis=-1)
    x = x + _layernorm(_L0_ffn_ref(_layernorm(x, axis=-1), L0_ffn_router_weight, L0_ffn_router_bias, L0_ffn_gate_up_proj, L0_ffn_gate_up_proj_bias, L0_ffn_down_proj, L0_ffn_down_proj_bias), axis=-1)
    return x

_drawn_inputs = setup_inputs


def setup_inputs(seed=0):
    import zlib

    import numpy as np

    out = dict(_drawn_inputs(seed))
    spreads = {}
    factors = {}
    for name, (base, spread) in spreads.items():
        noise = np.random.default_rng([zlib.crc32(name.encode()), seed]).standard_normal(out[name].shape)
        drawn = base * np.exp(spread * noise) if base else spread * noise
        out[name] = jnp.asarray(drawn.astype(out[name].dtype))
    for name, factor in factors.items():
        out[name] = (out[name] * factor).astype(out[name].dtype)
    return out
```

```python
from contextlib import ExitStack

import numpy as np

import concourse.bass as bass
from concourse import mybir

F32 = mybir.dt.float32
F32R = mybir.dt.float32r
ALU = mybir.AluOpType
ACT = mybir.ActivationFunctionType
AX_X = mybir.AxisListType.X

P = 128
B, T, M = 4, 256, 256
H, D = 16, 128
E, DF, TOP = 16, 256, 4
N = B * T
KM = M // P
TILES = N // P
HALF = N // 2
GROUPS = H // 2
PAIRS = 2 * B
QK_CHUNKS = 8
EPS = 1e-5
NEG = -1e30
ALPHA, LIMIT = 1.702, 7.0
SENTINEL = -3.0e38
FILL = 3.0e38


def pair_head(p):
    return (p // 2) % 2


def pair_batch(p):
    return 2 * (p // 4) + p % 2


def block_kernel(nc, x_d, wq_d, wk_d, wv_d, wo_d, rw_d, rb_d, gu_d, gub_d, dn_d, dnb_d,
                 rope_cos_d, rope_sin_d, mask_d, ident_d, out_d):
    ctx = ExitStack()
    with ctx:
        def sb(name, shape, dt=F32):
            return ctx.enter_context(nc.sbuf_tensor(name, shape, dt))

        def sem(name):
            return ctx.enter_context(nc.semaphore(name))

        x = sb("x", [P, TILES, M])
        xn = sb("xn", [P, TILES, M])
        xT_h = sb("xT_h", [P, KM, N], F32R)
        xT_l = sb("xT_l", [P, KM, N], F32R)
        attn = sb("attn", [P, TILES, M])
        moe = sb("moe", [P, TILES, M])
        rope_cos = sb("rope_cos", [P, T])
        rope_sin = sb("rope_sin", [P, T])
        mask = sb("mask", [P, T])
        ident = sb("ident", [P, P])
        stats = sb("stats", [P, TILES, 6])
        mean_var = sb("mean_var", [P, TILES, 2])
        var_eps = sb("var_eps", [P, TILES])
        rstd = sb("rstd", [P, TILES])
        minus_half = sb("minus_half", [P, TILES])

        raw_qk = [sb(f"raw_qk{a}", [P, 2, KM, D]) for a in range(2)]
        qk_h = [sb(f"qk_h{a}", [P, 2, KM, D], F32R) for a in range(2)]
        qk_l = [sb(f"qk_l{a}", [P, 2, KM, D], F32R) for a in range(2)]
        raw_v = sb("raw_v", [P, KM, 2 * D])
        wv_h = sb("wv_h", [P, KM, 2 * D], F32R)
        wv_l = sb("wv_l", [P, KM, 2 * D], F32R)
        raw_o = [sb(f"raw_o{a}", [P, M]) for a in range(2)]
        wo_h = [sb(f"wo_h{a}", [P, M], F32R) for a in range(2)]
        wo_l = [sb(f"wo_l{a}", [P, M], F32R) for a in range(2)]
        qkT = sb("qkT", [P, 2, 4, HALF])
        V = sb("V", [P, B, 2, 2 * D])
        by_cos = sb("by_cos", [P, 2, HALF])
        by_sin = sb("by_sin", [P, 2, HALF])
        score = sb("score", [P, 2, P + T])
        row_bias = sb("row_bias", [P, 2, 2])
        row_sum = sb("row_sum", [P, 2, 2])
        row_rec = sb("row_rec", [P, 2, 2])
        prob = sb("prob", [P, 2, P + T])
        probT = sb("probT", [P, P + T])
        oT_h = sb("oT_h", [P, 2, T], F32R)
        oT_l = sb("oT_l", [P, 2, T], F32R)

        raw_gu = sb("raw_gu", [P, KM, 2 * DF])
        gu_h = [sb(f"gu_h{r}", [P, KM, 2, P], F32R) for r in range(2)]
        gu_l = [sb(f"gu_l{r}", [P, KM, 2, P], F32R) for r in range(2)]
        raw_dn = sb("raw_dn", [P, 2, M])
        dn_h = sb("dn_h", [P, 2, M], F32R)
        dn_l = sb("dn_l", [P, 2, M], F32R)
        gub_rows = sb("gub_rows", [2 * E, 2 * P])
        gate_bias = sb("gate_bias", [P, 2 * E])
        up_bias = sb("up_bias", [P, 2 * E])
        dnb = sb("dnb", [E, M])
        gate = sb("gate", [P, 2, HALF])
        glu = sb("glu", [P, 2, HALF])
        up = sb("up", [P, 2, HALF])
        act = sb("act", [P, 2, HALF])
        actT_h = sb("actT_h", [P, 2, N], F32R)
        actT_l = sb("actT_l", [P, 2, N], F32R)

        rw = sb("rw", [E, M])
        rwT_h = sb("rwT_h", [P, KM, E], F32R)
        rwT_l = sb("rwT_l", [P, KM, E], F32R)
        rb = sb("rb", [P, E])
        logits = sb("logits", [P, TILES, E + 8])
        best = sb("best", [P, TILES, 8])
        top1 = sb("top1", [P, TILES])
        marked = sb("marked", [P, TILES, E + 8])
        chosen = sb("chosen", [P, TILES, E])
        shifted = sb("shifted", [P, TILES, E])
        expo = sb("expo", [P, TILES, E])
        weight = sb("weight", [P, TILES, E])
        wsum = sb("wsum", [P, TILES])
        wrec = sb("wrec", [P, TILES])
        route = sb("route", [P, TILES, E])
        routeT = sb("routeT", [E, N])

        bank = [ctx.enter_context(nc.psum_tensor(f"bank{i}", [P, 512], F32)) for i in range(8)]
        ps_qk = bank[0:2]
        ps_s, ps_pT, ps_oT, ps_v = bank[2:6]
        ps_r = bank[6:8]
        ps_gu = [bank[0:2], bank[2:4]]
        ps_dn = [bank[4:6], bank[6:8]]

        dma_x = [sem(f"dma_x{u}") for u in range(4)]
        dma_ident = sem("dma_ident")
        dma_rope = sem("dma_rope")
        dma_mask = sem("dma_mask")
        dma_small = sem("dma_small")
        dma_qk = [sem(f"dma_qk{a}") for a in range(2)]
        dma_v = sem("dma_v")
        dma_o = [sem(f"dma_o{a}") for a in range(2)]
        dma_gu = sem("dma_gu")
        dma_dn = sem("dma_dn")
        dma_out = sem("dma_out")

        pool_const = sem("pool_const")
        pool_rstd = sem("pool_rstd")
        pool_sin = sem("pool_sin")
        pool_qk = [sem(f"pool_qk{a}") for a in range(2)]
        pool_v = sem("pool_v")
        pool_o = [sem(f"pool_o{a}") for a in range(2)]
        pool_gu = [sem(f"pool_gu{r}") for r in range(2)]
        pool_dn = sem("pool_dn")
        pool_act = sem("pool_act")

        act_xT = sem("act_xT")
        act_swap = sem("act_swap")
        act_exp = sem("act_exp")
        act_pT = sem("act_pT")
        act_v = sem("act_v")
        act_oT = sem("act_oT")
        act_qk = [sem(f"act_qk{a}") for a in range(2)]
        act_wv = sem("act_wv")
        act_wo = [sem(f"act_wo{a}") for a in range(2)]
        act_gu = [sem(f"act_gu{r}") for r in range(2)]
        act_dn = sem("act_dn")
        act_glu = sem("act_glu")
        act_act = sem("act_act")
        act_small = sem("act_small")

        dve_stat = sem("dve_stat")
        dve_var = sem("dve_var")
        dve_xn = sem("dve_xn")
        dve_x1 = sem("dve_x1")
        dve_xT = sem("dve_xT")
        dve_cos = sem("dve_cos")
        dve_rope = sem("dve_rope")
        dve_max = sem("dve_max")
        dve_rec = sem("dve_rec")
        dve_norm = sem("dve_norm")
        dve_oT = sem("dve_oT")
        dve_attn = sem("dve_attn")
        dve_small = sem("dve_small")
        dve_route = sem("dve_route")
        dve_routeT = sem("dve_routeT")
        dve_gate = sem("dve_gate")
        dve_up = sem("dve_up")
        dve_act = sem("dve_act")
        dve_moe = sem("dve_moe")
        dve_out = sem("dve_out")

        pe_xT = sem("pe_xT")
        pe_qk = sem("pe_qk")
        pe_s = sem("pe_s")
        pe_pT = sem("pe_pT")
        pe_oT = sem("pe_oT")
        pe_v = sem("pe_v")
        pe_r = sem("pe_r")
        pe_small = sem("pe_small")
        pe_logits = sem("pe_logits")
        pe_routeT = sem("pe_routeT")
        pe_dnb = sem("pe_dnb")
        pe_gu = sem("pe_gu")
        pe_dn = sem("pe_dn")

        def step_rc(e, q):
            return (q % 2, q // 2) if isinstance(e, int) and e == 0 else (q // 2, q % 2)

        BETWEEN_EARLY = [("a", 0), ("a", 1), ("b", 0), ("b", 1)]
        BETWEEN = [("c", 0), ("c", 1), ("a", 2), ("a", 3), ("b", 2), ("b", 3), ("c", 2), ("c", 3)]
        POWERS = [step for step in BETWEEN_EARLY + BETWEEN if step[0] != "c"]
        V_CHUNK = {1: (0, 2), 2: (0, 3), 5: (1, 0), 6: (1, 1)}

        x_rows = x_d.rearrange("b (s p) m -> p (b s) m", p=P)
        out_rows = out_d.rearrange("b (s p) m -> p (b s) m", p=P)
        wq_cols = wq_d.rearrange("(k p) h d -> h p k d", p=P)
        wk_cols = wk_d.rearrange("(k p) h d -> h p k d", p=P)
        wv_cols = wv_d.rearrange("(k p) (g a) d -> g p k (a d)", p=P, a=2)
        gu_rows = gu_d.rearrange("e (k p) c -> e p k c", p=P)
        dn_rows = dn_d.rearrange("e (k p) m -> e p k m", p=P)

        block = ctx.enter_context(nc.Block())

        @block.sync
        def _(sp):
            for u in range(4):
                sp.dma_start(x[:, 2 * u:2 * u + 2, :], x_rows[:, 2 * u:2 * u + 2, :]).then_inc(dma_x[u], 16)
                if u == 0:
                    sp.dma_start(ident[:, :], ident_d).then_inc(dma_ident, 16)

            def load_qk(a, g):
                sp.dma_start(raw_qk[a][:, 0, :, :], wq_cols[2 * g + a]).then_inc(dma_qk[a], 16)
                sp.dma_start(raw_qk[a][:, 1, :, :], wk_cols[2 * g + a]).then_inc(dma_qk[a], 16)

            def load_v(g):
                sp.dma_start(raw_v[:, :, :], wv_cols[g]).then_inc(dma_v, 16)

            def load_o(a, g):
                sp.dma_start(raw_o[a][:, :], wo_d[2 * g + a]).then_inc(dma_o[a], 16)

            load_qk(0, 0)
            sp.dma_start(rope_cos[:, :], rope_cos_d).then_inc(dma_rope, 16)
            sp.dma_start(rope_sin[:, :], rope_sin_d).then_inc(dma_rope, 16)
            load_qk(1, 0)
            load_v(0)
            sp.dma_start(mask[:, :], mask_d).then_inc(dma_mask, 16)
            load_o(0, 0)
            load_o(1, 0)
            sp.dma_start(rw[:, :], rw_d).then_inc(dma_small, 16)
            sp.dma_start(rb[:, :], rb_d.partition_broadcast(P)).then_inc(dma_small, 16)
            sp.dma_start(gub_rows[:, :], gub_d.rearrange("e (r c) -> (e r) c", r=2)).then_inc(dma_small, 16)
            sp.dma_start(dnb[:, :], dnb_d).then_inc(dma_small, 16)
            with sp.Fori(1, GROUPS) as g:
                sp.wait_ge(pool_qk[0], g)
                load_qk(0, g)
                sp.wait_ge(pool_qk[1], g)
                load_qk(1, g)
                sp.wait_ge(pool_v, g)
                load_v(g)
                sp.wait_ge(pool_o[1], g)
                load_o(1, g)
                sp.wait_ge(pool_o[0], g)
                load_o(0, g)
            sp.dma_start(raw_gu[:, :, :], gu_rows[0]).then_inc(dma_gu, 16)
            sp.dma_start(raw_dn[:, :, :], dn_rows[0]).then_inc(dma_dn, 16)
            with sp.Fori(1, E) as e:
                sp.wait_ge(pool_gu[0], e)
                sp.wait_ge(pool_gu[1], e)
                sp.dma_start(raw_gu[:, :, :], gu_rows[e]).then_inc(dma_gu, 16)
                sp.wait_ge(pool_dn, e)
                sp.dma_start(raw_dn[:, :, :], dn_rows[e]).then_inc(dma_dn, 16)
            for u in range(4):
                sp.wait_ge(dve_out, u + 1)
                sp.dma_start(out_rows[:, 2 * u:2 * u + 2, :], xn[:, 2 * u:2 * u + 2, :]).then_inc(dma_out, 16)
            sp.wait_ge(dma_out, 16 * 4)

        @block.gpsimd
        def _(pool):
            pool.memset(minus_half[:, :], -0.5).then_inc(pool_const, 1)
            pool.memset(attn[:, :, :], 0.0).then_inc(pool_const, 1)
            pool.memset(logits[:, :, E:E + 8], SENTINEL).then_inc(pool_const, 1)
            pool.wait_ge(pool_const, 1)

            def power(n, a, b):
                pool.wait_ge(dve_var, n + 1)
                pool.tensor_tensor(rstd[:, a:b], var_eps[:, a:b], minus_half[:, a:b], ALU.pow).then_inc(pool_rstd, 1)

            def low(out, raw, high, ready, n, done):
                pool.wait_ge(ready, n)
                pool.tensor_tensor(out, raw, high.bitcast(F32), ALU.subtract).then_inc(done, 1)

            def low_qk(a, g):
                low(qk_l[a][:, :, :, :], raw_qk[a][:, :, :, :], qk_h[a][:, :, :, :], act_qk[a], g + 1, pool_qk[a])

            def low_v(g):
                low(wv_l[:, :, :], raw_v[:, :, :], wv_h[:, :, :], act_wv, g + 1, pool_v)

            def low_o(a, g):
                low(wo_l[a][:, :], raw_o[a][:, :], wo_h[a][:, :], act_wo[a], g + 1, pool_o[a])

            def times_sine(n, w):
                pool.wait_ge(act_swap, n + 1)
                v = by_sin[:, w, :].rearrange("p (b t) -> p b t", b=2)
                pool.tensor_tensor(v, v, rope_sin[:, :].unsqueeze(1).broadcast_to([P, 2, T]), ALU.mult).then_inc(pool_sin, 1)

            def slot(g, p, last):
                if not (last and p >= 2):
                    times_sine(QK_CHUNKS * g + p + 6, p % 2)
                if p == 1:
                    low_o(1, g)
                if not last:
                    if p == 0:
                        low_qk(0, g + 1)
                    if p == 2:
                        low_qk(1, g + 1)
                    if p == 3:
                        low_v(g + 1)
                    if p == 7:
                        low_o(0, g + 1)

            for u in range(4):
                power(u, 2 * u, 2 * u + 2)
                if u == 0:
                    low_qk(0, 0)
                if u == 1:
                    low_qk(1, 0)
            pool.wait_ge(dma_rope, 32)
            for n in range(6):
                times_sine(n, n % 2)
                if n == 1:
                    low_v(0)
                if n == 2:
                    low_o(0, 0)
            with pool.Fori(0, GROUPS - 1) as g:
                for p in range(PAIRS):
                    slot(g, p, False)
            for p in range(PAIRS):
                slot(GROUPS - 1, p, True)

            def gu_view(r):
                return raw_gu[:, :, :].rearrange("p k (d s) -> p k s d", s=2)[:, :, :, r * P:(r + 1) * P]

            def low_gu(r, e):
                low(gu_l[r][:, :, :, :], gu_view(r), gu_h[r][:, :, :, :], act_gu[r], e + 1, pool_gu[r])

            def low_dn(e):
                low(dn_l[:, :, :], raw_dn[:, :, :], dn_h[:, :, :], act_dn, e + 1, pool_dn)

            for i, (_, u) in enumerate(POWERS):
                power(4 + i, 2 * u, 2 * u + 2)
                if i == len(BETWEEN_EARLY) - 1:
                    low_gu(0, 0)
                    low_gu(1, 0)
            low_dn(0)

            def low_act(e, q):
                r, c = step_rc(e, q)
                pool.wait_ge(act_act, 4 * e + q + 1)
                pool.tensor_tensor(actT_l[:, r, c * HALF:(c + 1) * HALF], act[:, q % 2, :],
                                   actT_h[:, r, c * HALF:(c + 1) * HALF].bitcast(F32),
                                   ALU.subtract).then_inc(pool_act, 1)

            def expert(e, last):
                low_gu(1, e)
                if not last:
                    low_gu(0, e + 1)
                low_act(e, 0)
                low_act(e, 1)
                low_dn(e)
                low_act(e, 2)
                low_act(e, 3)

            for q in range(4):
                low_act(0, q)
                if q == 2:
                    low_gu(0, 1)
            with pool.Fori(1, E - 1) as e:
                expert(e, False)
            expert(E - 1, True)
            for u in range(4):
                power(4 + len(POWERS) + u, 2 * u, 2 * u + 2)

        @block.scalar
        def _(sc):
            def copy(out, in_):
                return sc.activation(out, in_, ACT.Copy)

            def high_qk(a, g, free=True):
                sc.wait_ge(dma_qk[a], 32 * g + 32)
                if free:
                    sc.wait_ge(pe_qk, QK_CHUNKS * g - 2 + 2 * a)
                copy(qk_h[a][:, :, :, :], raw_qk[a][:, :, :, :]).then_inc(act_qk[a], 1)

            def high_v(g, free=True):
                sc.wait_ge(dma_v, 16 * g + 16)
                if free:
                    sc.wait_ge(pe_v, 4 * g)
                copy(wv_h[:, :, :], raw_v[:, :, :]).then_inc(act_wv, 1)

            def high_o(a, g, free=True):
                sc.wait_ge(dma_o[a], 16 * g + 16)
                if free:
                    sc.wait_ge(pe_r, PAIRS * g - (0 if a else 2))
                copy(wo_h[a][:, :], raw_o[a][:, :]).then_inc(act_wo[a], 1)

            def swap(n, w):
                sc.wait_ge(dve_cos, n + 1)
                sc.wait_ge(dve_rope, n - 1) if not (isinstance(n, int) and n < 2) else None
                copy(by_sin[0:64, w, :], ps_qk[w][64:128, :])
                copy(by_sin[64:128, w, :], ps_qk[w][0:64, :]).then_inc(act_swap, 1)

            def softmax_exp(g, p):
                k = PAIRS * g + p
                sc.wait_ge(dve_max, k + 1)
                if not (isinstance(k, int) and k < 2):
                    sc.wait_ge(pe_pT, k - 1)
                for i, (lo, hi) in enumerate([(0, P), (P, P + T)]):
                    e = sc.activation(prob[:, p % 2, lo:hi], score[:, p % 2, lo:hi], ACT.Exp,
                                      bias=row_bias[:, p % 2, i:i + 1], scale=-1.0,
                                      accum_out=row_sum[:, p % 2, i:i + 1])
                e.then_inc(act_exp, 1)

            def values(m, b, free):
                sc.wait_ge(pe_v, m + 1)
                if free is not None:
                    sc.wait_ge(pe_oT, free)
                copy(V[:, b, :, :], ps_v[:, :].rearrange("p (s c) -> p s c", s=2)).then_inc(act_v, 1)

            def oT_high(g, p):
                k = PAIRS * g + p
                sc.wait_ge(pe_oT, k + 1)
                if not (isinstance(k, int) and k < 2):
                    sc.wait_ge(pe_r, k - 1)
                copy(oT_h[:, p % 2, :], ps_oT[:, 0:T]).then_inc(act_oT, 1)

            def slot(g, p, first, last):
                if not (first and p == 0):
                    oT_high(g - (p == 0), (p - 1) % PAIRS)
                if not (last and p == PAIRS - 1):
                    softmax_exp(g + (p == PAIRS - 1), (p + 1) % PAIRS)
                sc.wait_ge(pe_pT, PAIRS * g + p + 1)
                copy(probT[:, :], ps_pT[:, 0:P + T]).then_inc(act_pT, 1)
                if not (last and p >= 2):
                    swap(QK_CHUNKS * g + p + 6, p % 2)
                if p in V_CHUNK and not (last and V_CHUNK[p][0]):
                    dg, b = V_CHUNK[p]
                    free = None if first and not dg else PAIRS * (g + dg - 1) + 4 * (b // 2) + 2 + b % 2 + 1
                    values(4 * (g + dg) + b, b, free)
                if p == 1:
                    high_o(1, g, not first)
                if not last:
                    if p == 0:
                        high_qk(0, g + 1)
                    if p == 2:
                        high_qk(1, g + 1)
                    if p == 3:
                        high_v(g + 1)
                    if p == 7:
                        high_o(0, g + 1)

            def xT_high(u):
                sc.wait_ge(pe_xT, u + 1)
                copy(xT_h[:, :, u * T:(u + 1) * T], bank[2 + u][:, :].rearrange("p (k t) -> p k t", k=KM)).then_inc(act_xT, 1)

            high_qk(0, 0, False)
            high_qk(1, 0, False)
            xT_high(0)
            xT_high(1)
            high_v(0, False)
            high_o(0, 0, False)
            xT_high(2)
            xT_high(3)
            for n in range(6):
                swap(n, n % 2)
                if n == 2:
                    values(0, 0, None)
                if n == 3:
                    values(1, 1, None)
            softmax_exp(0, 0)
            for p in range(PAIRS):
                slot(0, p, True, False)
            with sc.Fori(1, GROUPS - 1) as g:
                for p in range(PAIRS):
                    slot(g, p, False, False)
            for p in range(PAIRS):
                slot(GROUPS - 1, p, False, True)
            oT_high(GROUPS - 1, PAIRS - 1)

            def gu_view(r):
                return raw_gu[:, :, :].rearrange("p k (d s) -> p k s d", s=2)[:, :, :, r * P:(r + 1) * P]

            def high_gu(r, e, free=True):
                sc.wait_ge(dma_gu, 16 * e + 16)
                if free:
                    sc.wait_ge(pe_gu, 3 if isinstance(e, int) and e == 1 and r == 0 else 4 * e - 2 + 2 * r)
                for k in range(KM):
                    c = copy(gu_h[r][:, k, :, :], gu_view(r)[:, k, :, :])
                c.then_inc(act_gu[r], 1)

            def high_dn(e, free=True):
                sc.wait_ge(dma_dn, 16 * e + 16)
                if free:
                    sc.wait_ge(pe_dn, 4 * e)
                copy(dn_h[:, :, :], raw_dn[:, :, :]).then_inc(act_dn, 1)

            def xT_high_2(u, bank_of):
                sc.wait_ge(pe_xT, 4 + u + 1)
                copy(xT_h[:, :, u * T:(u + 1) * T], bank_of[:, :].rearrange("p (k t) -> p k t", k=KM)).then_inc(act_xT, 1)

            def gelu(e, q, first):
                s = 4 * e + q
                sc.wait_ge(dve_gate, s + 1)
                if not (first and q < 2):
                    sc.wait_ge(dve_act, s - 1)
                sc.activation(glu[:, q % 2, :], gate[:, q % 2, :], ACT.Gelu_apprx_sigmoid).then_inc(act_glu, 1)

            def act_high(e, q, first):
                s = 4 * e + q
                r, c = step_rc(e, q)
                sc.wait_ge(dve_act, s + 1)
                if not first:
                    sc.wait_ge(pe_dn, 4 * (e - 1) + 2 * c + 2)
                copy(actT_h[:, r, c * HALF:(c + 1) * HALF], act[:, q % 2, :]).then_inc(act_act, 1)

            def expert(e, last):
                high_gu(1, e)
                gelu(e, 0, False)
                gelu(e, 1, False)
                if not last:
                    high_gu(0, e + 1)
                act_high(e, 0, False)
                gelu(e, 2, False)
                act_high(e, 1, False)
                high_dn(e)
                act_high(e, 2, False)
                gelu(e, 3, False)
                act_high(e, 3, False)

            high_gu(0, 0, False)
            high_gu(1, 0, False)
            high_dn(0, False)
            xT_high_2(0, bank[0])
            xT_high_2(1, bank[1])
            gelu(0, 0, True)
            act_high(0, 0, True)
            gelu(0, 1, True)
            act_high(0, 1, True)
            xT_high_2(2, bank[4])
            xT_high_2(3, bank[5])
            sc.wait_ge(dve_small, 8)
            sc.activation(expo[:, :, :], shifted[:, :, :], ACT.Exp).then_inc(act_small, 1)
            gelu(0, 2, True)
            act_high(0, 2, True)
            gelu(0, 3, True)
            high_gu(0, 1)
            act_high(0, 3, True)
            with sc.Fori(1, E - 1) as e:
                expert(e, False)
            expert(E - 1, True)

        @block.vector
        def _(dve):
            count = {"stat": 0, "var": 0}
            var_at = {}

            def chain(ins):
                count["stat"] += 1
                ins.then_inc(dve_stat, 1)
                dve.wait_ge(dve_stat, count["stat"])

            def row_stats(src, tiles):
                for t in tiles:
                    s = dve.bn_stats(stats[:, t, :], src[:, t, :])
                chain(s)
                for t in tiles:
                    s = dve.bn_aggr(mean_var[:, t, :], stats[:, t, :])
                chain(s)
                a, b = tiles[0], tiles[-1] + 1
                dve.tensor_scalar(var_eps[:, a:b], mean_var[:, a:b, 1], EPS, None, ALU.add).then_inc(dve_var, 1)
                count["var"] += 1
                return count["var"]

            def normalise(out, src, t):
                return dve.tensor_scalar(out[:, t, :], src[:, t, :], mean_var[:, t, 0:1], rstd[:, t:t + 1],
                                         ALU.subtract, ALU.mult)

            def xT_low(u, bank_of):
                dve.wait_ge(act_xT, u + 1)
                c = (u % 4) * T
                dve.tensor_tensor(xT_l[:, :, c:c + T], bank_of[:, :].rearrange("p (k t) -> p k t", k=KM),
                                  xT_h[:, :, c:c + T].bitcast(F32), ALU.subtract).then_inc(dve_xT, 1)

            for u in range(4):
                dve.wait_ge(dma_x[u], 16)
                n = row_stats(x, [2 * u, 2 * u + 1])
                dve.wait_ge(pool_rstd, n)
                normalise(xn, x, 2 * u)
                normalise(xn, x, 2 * u + 1).then_inc(dve_xn, 1)
                if u >= 1:
                    xT_low(u - 1, bank[2 + u - 1])
            xT_low(3, bank[5])

            def cosine(n, w):
                dve.wait_ge(pe_qk, n + 1)
                if not (isinstance(n, int) and n < 2):
                    dve.wait_ge(dve_rope, n - 1)
                v = by_cos[:, w, :].rearrange("p (b t) -> p b t", b=2)
                dve.tensor_tensor(v, ps_qk[w][:, :].rearrange("p (b t) -> p b t", b=2),
                                  rope_cos[:, :].unsqueeze(1).broadcast_to([P, 2, T]), ALU.mult).then_inc(dve_cos, 1)

            def rotate(n, w, j, free):
                dve.wait_ge(pool_sin, n + 1)
                dve.wait_ge(dve_cos, n + 1)
                if free is not None:
                    dve.wait_ge(pe_s, free)
                dve.tensor_tensor(qkT[:, w, j, :], by_cos[:, w, :], by_sin[:, w, :], ALU.add).then_inc(dve_rope, 1)

            def await_scores(g, p):
                k = PAIRS * g + p
                dve.wait_ge(pe_s, k + 1)
                if not (isinstance(k, int) and k < 2):
                    dve.wait_ge(act_exp, k - 1)

            def row_max(p):
                for i, (lo, hi) in enumerate([(0, P), (P, P + T)]):
                    m = dve.tensor_tensor_reduce(score[:, p % 2, lo:hi], ps_s[:, lo:hi], mask[:, P:T] if i == 0 else mask[:, :],
                                                 -1.0 / D, FILL, ALU.add, ALU.min, row_bias[:, p % 2, i:i + 1])
                m.then_inc(dve_max, 1)

            def normalise_prob(g, p):
                k = PAIRS * g + p
                dve.wait_ge(act_exp, k + 1)
                dve.reciprocal(row_rec[:, p % 2, :], row_sum[:, p % 2, :]).then_inc(dve_rec, 1)
                dve.wait_ge(dve_rec, k + 1)
                for i, (lo, hi) in enumerate([(0, P), (P, P + T)]):
                    m = dve.tensor_scalar(prob[:, p % 2, lo:hi], prob[:, p % 2, lo:hi], row_rec[:, p % 2, i:i + 1],
                                          None, ALU.mult)
                m.then_inc(dve_norm, 1)

            def oT_low(g, p):
                dve.wait_ge(act_oT, PAIRS * g + p + 1)
                dve.tensor_tensor(oT_l[:, p % 2, :], ps_oT[:, 0:T], oT_h[:, p % 2, :].bitcast(F32),
                                  ALU.subtract).then_inc(dve_oT, 1)

            def add_attn(g, p):
                dve.wait_ge(pe_r, PAIRS * g + p + 1)
                b = pair_batch(p)
                v = attn[:, 2 * b:2 * b + 2, :]
                dve.tensor_tensor(v, ps_r[b % 2][:, :].rearrange("p (s m) -> p s m", s=2), v, ALU.add).then_inc(dve_attn, 1)

            def slot(g, p, first, last):
                if not (last and p == PAIRS - 1):
                    await_scores(g + (p == PAIRS - 1), (p + 1) % PAIRS)
                if not (first and p == 0):
                    oT_low(g - (p == 0), (p - 1) % PAIRS)
                if not (last and p == PAIRS - 1):
                    row_max((p + 1) % PAIRS)
                if not (last and p >= 2):
                    cosine(QK_CHUNKS * g + p + 6, p % 2)
                if not (last and p == PAIRS - 1):
                    normalise_prob(g + (p == PAIRS - 1), (p + 1) % PAIRS)
                if not (last and p >= 3):
                    n = QK_CHUNKS * g + p + 5
                    j = ((p + 5) // 2) % 4
                    free = None if first and (p + 5) // 2 < 4 else PAIRS * g + 2 * ((p + 5) // 2) - 6
                    rotate(n, (p + 1) % 2, j, free)
                if not (first and p < 2) and pair_head((p - 2) % PAIRS):
                    add_attn(g - (p < 2), (p - 2) % PAIRS)

            for n in range(6):
                if n == 0:
                    dve.wait_ge(dma_rope, 32)
                cosine(n, n % 2)
                if n >= 1:
                    rotate(n - 1, (n - 1) % 2, (n - 1) // 2, None)
            await_scores(0, 0)
            dve.wait_ge(dma_mask, 16)
            row_max(0)
            normalise_prob(0, 0)
            dve.wait_ge(pool_const, 3)
            for p in range(PAIRS):
                slot(0, p, True, False)
            with dve.Fori(1, GROUPS - 1) as g:
                for p in range(PAIRS):
                    slot(g, p, False, False)
            def between(kind, u):
                tiles = [2 * u, 2 * u + 1]
                if kind == "a":
                    dve.wait_ge(dve_attn, 4 * (GROUPS - 1) + u + 1)
                    var_at["a", u] = row_stats(attn, tiles)
                if kind == "b":
                    dve.wait_ge(pool_rstd, var_at["a", u])
                    for t in tiles:
                        m = normalise(attn, attn, t)
                    chain(m)
                    v = x[:, 2 * u:2 * u + 2, :]
                    chain(dve.tensor_tensor(v, attn[:, 2 * u:2 * u + 2, :], v, ALU.add))
                    var_at["b", u] = row_stats(x, tiles)
                if kind == "c":
                    dve.wait_ge(pool_rstd, var_at["b", u])
                    for t in tiles:
                        m = normalise(xn, x, t)
                    m.then_inc(dve_xn, 1)

            def small_tables():
                dve.wait_ge(pe_small, 1)
                dve.tensor_copy(gate_bias[:, :], bank[0][:, 0:2 * E])
                dve.tensor_scalar(up_bias[:, :], bank[0][:, 2 * E:4 * E], 1.0, None, ALU.add)
                dve.tensor_copy(rwT_h[:, :, :], bank[0][:, 4 * E:6 * E].rearrange("p (k e) -> p k e", k=KM)).then_inc(dve_small, 1)
                dve.wait_ge(dve_small, 1)
                dve.tensor_tensor(rwT_l[:, :, :], bank[0][:, 4 * E:6 * E].rearrange("p (k e) -> p k e", k=KM),
                                  rwT_h[:, :, :].bitcast(F32), ALU.subtract).then_inc(dve_small, 1)

            for p in range(PAIRS):
                slot(GROUPS - 1, p, False, True)
                if p == 3:
                    small_tables()
                if p == 5:
                    for kind, u in BETWEEN_EARLY[:2]:
                        between(kind, u)
                if p == 6:
                    for kind, u in BETWEEN_EARLY[2:]:
                        between(kind, u)
            oT_low(GROUPS - 1, PAIRS - 1)
            for kind, u in BETWEEN[:2]:
                between(kind, u)
            add_attn(GROUPS - 1, PAIRS - 2)
            add_attn(GROUPS - 1, PAIRS - 1)

            for kind, u in BETWEEN[2:4]:
                between(kind, u)
            xT_low(4, bank[0])
            xT_low(5, bank[1])
            for kind, u in BETWEEN[4:]:
                between(kind, u)

            def router():
                dve.wait_ge(pe_logits, 1)
                dve.wait_ge(dma_small, 64)
                dve.tensor_tensor(logits[:, :, 0:E], bank[6][:, 0:TILES * E].rearrange("p (t e) -> p t e", e=E),
                                  rb[:, :].unsqueeze(1).broadcast_to([P, TILES, E]), ALU.add).then_inc(dve_small, 1)
                dve.wait_ge(dve_small, 3)
                for t in range(TILES):
                    m = dve.max(best[:, t, :], logits[:, t, 0:E])
                m.then_inc(dve_small, 1)
                dve.wait_ge(dve_small, 4)
                dve.memset(best[:, :, TOP:8], SENTINEL).then_inc(dve_small, 1)
                dve.wait_ge(dve_small, 5)
                for t in range(TILES):
                    m = dve.match_replace(marked[:, t, :], best[:, t, :], logits[:, t, :], FILL)
                m.then_inc(dve_small, 1)
                dve.wait_ge(dve_small, 6)
                dve.tensor_tensor(chosen[:, :, :], marked[:, :, 0:E], logits[:, :, 0:E], ALU.not_equal).then_inc(dve_small, 1)
                dve.tensor_tensor(shifted[:, :, :], logits[:, :, 0:E], best[:, :, 0:1].broadcast_to([P, TILES, E]),
                                  ALU.subtract).then_inc(dve_small, 1)
                dve.wait_ge(act_small, 1)
                dve.wait_ge(dve_small, 8)
                dve.tensor_tensor(weight[:, :, :], expo[:, :, :], chosen[:, :, :], ALU.mult).then_inc(dve_small, 1)
                dve.wait_ge(dve_small, 9)
                dve.tensor_reduce(wsum[:, :], weight[:, :, :], AX_X, ALU.add).then_inc(dve_small, 1)
                dve.wait_ge(dve_small, 10)
                dve.reciprocal(wrec[:, :], wsum[:, :]).then_inc(dve_small, 1)
                dve.wait_ge(dve_small, 11)
                dve.tensor_tensor(route[:, :, :], weight[:, :, :], wrec[:, :].unsqueeze(2).broadcast_to([P, TILES, E]),
                                  ALU.mult).then_inc(dve_route, 1)
            def router_part_2():
                for c in range(2):
                    dve.wait_ge(pe_routeT, c + 1)
                    dve.tensor_copy(routeT[:, c * HALF:(c + 1) * HALF], bank[4 + c][0:E, :]).then_inc(dve_routeT, 1)
                for u in range(4):
                    dve.wait_ge(pe_dnb, u + 1)
                    dve.tensor_copy(moe[:, 2 * u:2 * u + 2, :], bank[4 + u][:, :].rearrange("p (s m) -> p s m", s=2)).then_inc(dve_moe, 1)
                dve.wait_ge(dve_moe, 4)

            def add_moe(e, c):
                for w in range(2):
                    dve.wait_ge(pe_dn, 4 * e + 2 * c + w + 1)
                    if not (isinstance(e, int) and e == 0):
                        dve.wait_ge(dve_moe, 4 * e + 2 * c + w + 1)
                    for s in range(2):
                        t = 4 * c + 2 * w + s
                        m = dve.scalar_tensor_tensor(out=moe[:, t, :], in0=ps_dn[c][w][:, s * M:(s + 1) * M],
                                                     scalar=route[:, t, bass.ds(e, 1)], in1=moe[:, t, :],
                                                     op0=ALU.mult, op1=ALU.add)
                    m.then_inc(dve_moe, 1)

            def clamp(e, q, first):
                s = 4 * e + q
                r, _ = step_rc(e, q)
                dve.wait_ge(pe_gu, s + 1)
                if not (first and q < 2):
                    dve.wait_ge(act_glu, s - 1)
                dve.tensor_scalar(gate[:, q % 2, :], ps_gu[q % 2][0][:, :], gate_bias[:, bass.ds(2 * e + r, 1)], LIMIT,
                                  ALU.add, ALU.min).then_inc(dve_gate, 1)
                if not (first and q < 2):
                    dve.wait_ge(dve_act, s - 1)
                dve.tensor_scalar(up[:, q % 2, :], ps_gu[q % 2][1][:, :], up_bias[:, bass.ds(2 * e + r, 1)], 1.0 - LIMIT,
                                  ALU.add, ALU.max).then_inc(dve_up, 1)

            def gated(e, q, first):
                s = 4 * e + q
                dve.wait_ge(act_glu, s + 1)
                dve.wait_ge(dve_up, s + 1)
                if not (first and q < 2):
                    dve.wait_ge(pool_act, s - 1)
                dve.scalar_tensor_tensor(out=act[:, q % 2, :], in0=up[:, q % 2, :], scalar=1.0 + LIMIT,
                                         in1=glu[:, q % 2, :], op0=ALU.min, op1=ALU.mult).then_inc(dve_act, 1)

            def expert(e, first):
                for q in range(4):
                    clamp(e, q, first)
                    gated(e, q, first)
                    if q in (1, 2) and not first:
                        add_moe(e - 1, q - 1)

            for q in range(4):
                clamp(0, q, True)
                gated(0, q, True)
                if q == 1:
                    xT_low(6, bank[4])
                    xT_low(7, bank[5])
                    router()
            clamp(1, 0, False)
            gated(1, 0, False)
            router_part_2()
            for q in range(1, 4):
                clamp(1, q, False)
                gated(1, q, False)
                if q < 3:
                    add_moe(0, q - 1)
            with dve.Fori(2, E) as e:
                expert(e, False)

            def finish(u):
                dve.wait_ge(pool_rstd, var_at["out", u])
                for t in (2 * u, 2 * u + 1):
                    m = normalise(moe, moe, t)
                chain(m)
                dve.tensor_tensor(xn[:, 2 * u:2 * u + 2, :], moe[:, 2 * u:2 * u + 2, :], x[:, 2 * u:2 * u + 2, :],
                                  ALU.add).then_inc(dve_out, 1)

            for c in range(2):
                add_moe(E - 1, c)
                for u in (2 * c, 2 * c + 1):
                    dve.wait_ge(dve_moe, 4 * E + u + 1)
                    var_at["out", u] = row_stats(moe, [2 * u, 2 * u + 1])
                for u in (2 * c, 2 * c + 1):
                    finish(u)

        @block.tensor
        def _(pe):
            def product(out, pairs, first=True, last=True):
                terms = [t for lh, ll, rh, rl in pairs for t in ((lh, rh), (lh, rl), (ll, rh))]
                for i, (lhs, rhs) in enumerate(terms):
                    m = pe.matmul(out, lhs, rhs, start=first and i == 0, stop=last and i == len(terms) - 1,
                                  skip_group_check=not (first and last))
                return m

            def turn_rows(u, bank_of):
                for s in range(2):
                    for k in range(KM):
                        m = pe.transpose(bank_of[:, k * T + s * P:k * T + (s + 1) * P],
                                         xn[:, 2 * u + s, k * P:(k + 1) * P], ident[:, :])
                m.then_inc(pe_xT, 1)

            def qk_chunk(n, w, a, c, group, free):
                pe.wait_ge(pool_qk[a], group + 1)
                if free:
                    pe.wait_ge(act_swap, n - 1)
                cols = slice(c * HALF, (c + 1) * HALF)
                product(ps_qk[w][:, :], [(qk_h[a][:, w, k, :], qk_l[a][:, w, k, :], xT_h[:, k, cols], xT_l[:, k, cols])
                                         for k in range(KM)]).then_inc(pe_qk, 1)

            def v_chunk(m, b, group, free):
                pe.wait_ge(pool_v, group + 1)
                if free:
                    pe.wait_ge(act_v, m)
                for s in range(2):
                    cols = slice((2 * b + s) * P, (2 * b + s + 1) * P)
                    v = product(ps_v[:, s * T:(s + 1) * T], [(xT_h[:, k, cols], xT_l[:, k, cols], wv_h[:, k, :], wv_l[:, k, :])
                                                             for k in range(KM)])
                v.then_inc(pe_v, 1)

            def scores(g, p, free):
                j, o = p // 2, (p % 2) * T
                if p % 2 == 0:
                    pe.wait_ge(dve_rope, QK_CHUNKS * g + 2 * j + 2)
                if free:
                    pe.wait_ge(dve_max, PAIRS * g + p)
                pe.matmul(ps_s[:, 0:P], qkT[:, 0, j, o:o + P], qkT[:, 1, j, o:o + P], start=True, stop=True)
                pe.matmul(ps_s[:, P:P + T], qkT[:, 0, j, o + P:o + T], qkT[:, 1, j, o:o + T],
                          start=True, stop=True).then_inc(pe_s, 1)

            def turn_prob(g, p, free):
                pe.wait_ge(dve_norm, PAIRS * g + p + 1)
                if free:
                    pe.wait_ge(act_pT, PAIRS * g + p)
                for i in range(3):
                    m = pe.transpose(ps_pT[:, i * P:(i + 1) * P], prob[:, p % 2, i * P:(i + 1) * P], ident[:, :])
                m.then_inc(pe_pT, 1)

            def weigh_values(g, p, free):
                a, b = pair_head(p), pair_batch(p)
                pe.wait_ge(act_pT, PAIRS * g + p + 1)
                pe.wait_ge(act_v, 4 * g + b + 1)
                if free:
                    pe.wait_ge(dve_oT, PAIRS * g + p)
                pe.matmul(ps_oT[:, 0:T], V[:, b, 0, a * D:(a + 1) * D], probT[:, 0:T], start=True, stop=False,
                          skip_group_check=True)
                pe.matmul(ps_oT[:, P:T], V[:, b, 1, a * D:(a + 1) * D], probT[:, T:T + P], start=False, stop=True,
                          skip_group_check=True).then_inc(pe_oT, 1)

            def output_rows(g, p, first):
                a, b = pair_head(p), pair_batch(p)
                pe.wait_ge(dve_oT, PAIRS * g + p + 1)
                pe.wait_ge(pool_o[a], g + 1)
                if a == 0 and not (first and p < 2):
                    pe.wait_ge(dve_attn, 4 * g + 2 * (p // 4) + p % 2 - 1)
                for s in range(2):
                    m = product(ps_r[b % 2][:, s * M:(s + 1) * M],
                                [(oT_h[:, p % 2, s * P:(s + 1) * P], oT_l[:, p % 2, s * P:(s + 1) * P], wo_h[a][:, :], wo_l[a][:, :])],
                                first=(a == 0 and s == 0), last=(a == 1))
                m.then_inc(pe_r, 1)

            def slot(g, p, first, last):
                if not (last and p == PAIRS - 1):
                    scores(g + (p == PAIRS - 1), (p + 1) % PAIRS, True)
                if not (last and p >= 2):
                    unit = (p + 6) // 2
                    qk_chunk(QK_CHUNKS * g + p + 6, p % 2, unit % 2, (unit // 2) % 2, g + (unit >= 4), True)
                turn_prob(g, p, not (first and p == 0))
                if not (first and p == 0):
                    output_rows(g - (p == 0), (p - 1) % PAIRS, first and p != 0)
                if p in V_CHUNK and not (last and V_CHUNK[p][0]):
                    dg, b = V_CHUNK[p]
                    v_chunk(4 * (g + dg) + b, b, g + dg, True)
                weigh_values(g, p, not (first and p == 0))

            pe.wait_ge(dma_ident, 16)
            for u in range(4):
                pe.wait_ge(dve_xn, u + 1)
                turn_rows(u, bank[2 + u])
            for n in range(6):
                if n == 0:
                    pe.wait_ge(dve_xT, 2)
                if n == 4:
                    pe.wait_ge(dve_xT, 4)
                qk_chunk(n, n % 2, (n // 2) % 2, n // 4, 0, n >= 2)
                if n == 4:
                    v_chunk(0, 0, 0, False)
                if n == 5:
                    v_chunk(1, 1, 0, True)
            scores(0, 0, False)
            for p in range(PAIRS):
                slot(0, p, True, False)
            with pe.Fori(1, GROUPS - 1) as g:
                for p in range(PAIRS):
                    slot(g, p, False, False)
            for p in range(PAIRS):
                slot(GROUPS - 1, p, False, True)
                if p == 2:
                    pe.wait_ge(act_swap, QK_CHUNKS * GROUPS)
                    pe.wait_ge(dma_small, 64)
                    for s in range(2):
                        rows = gub_rows[:, :].rearrange("q (d s) -> q s d", s=2)[:, s, :]
                        pe.transpose(bank[0][:, s * 2 * E:(s + 1) * 2 * E], rows, ident[0:2 * E, 0:2 * E])
                    for k in range(KM):
                        m = pe.transpose(bank[0][:, (4 + k) * E:(5 + k) * E], rw[:, k * P:(k + 1) * P], ident[0:E, 0:E])
                    m.then_inc(pe_small, 1)
            output_rows(GROUPS - 1, PAIRS - 1, False)

            def gate_up(e, q, free):
                r, c = step_rc(e, q)
                pe.wait_ge(pool_gu[r], e + 1)
                if free:
                    pe.wait_ge(dve_up, 4 * e + q - 1)
                cols = slice(c * HALF, (c + 1) * HALF)
                for w in range(2):
                    m = product(ps_gu[q % 2][w][:, :],
                                [(gu_h[r][:, k, w, :], gu_l[r][:, k, w, :], xT_h[:, k, cols], xT_l[:, k, cols])
                                 for k in range(KM)])
                m.then_inc(pe_gu, 1)

            def down(e, c):
                if c == 0:
                    pe.wait_ge(pool_dn, e + 1)
                pe.wait_ge(pool_act, 4 * e + 2 + c + 1)
                for w in range(2):
                    pe.wait_ge(dve_moe, 4 * e + 2 * c + w + 1)
                    for s in range(2):
                        t = 4 * c + 2 * w + s
                        cols = slice(t * P, (t + 1) * P)
                        m = product(ps_dn[c][w][:, s * M:(s + 1) * M],
                                    [(actT_h[:, r, cols], actT_l[:, r, cols], dn_h[:, r, :], dn_l[:, r, :]) for r in range(2)])
                    m.then_inc(pe_dn, 1)

            def expert(e, first, last):
                for q in range(4):
                    gate_up(e, q, not (first and q < 2))
                    if q in (1, 2) and not first:
                        down(e - 1, q - 1)

            pe.wait_ge(dve_small, 2)
            for u in range(2):
                pe.wait_ge(dve_xn, 4 + u + 1)
                turn_rows(u, bank[u])
            pe.wait_ge(dve_xT, 6)
            gate_up(0, 0, False)
            gate_up(0, 1, False)
            for u in range(2, 4):
                pe.wait_ge(dve_xn, 4 + u + 1)
                turn_rows(u, bank[2 + u])
            pe.wait_ge(dve_xT, 8)
            for t in range(TILES):
                cols = slice(t * P, (t + 1) * P)
                m = product(bank[6][:, t * E:(t + 1) * E],
                            [(xT_h[:, k, cols], xT_l[:, k, cols], rwT_h[:, k, :], rwT_l[:, k, :]) for k in range(KM)])
            m.then_inc(pe_logits, 1)
            gate_up(0, 2, True)
            gate_up(0, 3, True)
            pe.wait_ge(dve_route, 1)
            for t in range(TILES):
                m = pe.transpose(bank[4 + t // 4][0:E, (t % 4) * P:(t % 4 + 1) * P], route[:, t, :], ident[:, :])
                if t % 4 == 3:
                    m.then_inc(pe_routeT, 1)
            gate_up(1, 0, True)
            pe.wait_ge(dve_routeT, 2)
            for t in range(TILES):
                m = pe.matmul(bank[4 + t // 2][:, (t % 2) * M:(t % 2 + 1) * M], routeT[:, t * P:(t + 1) * P], dnb[:, :],
                              start=True, stop=True)
                if t % 2 == 1:
                    m.then_inc(pe_dnb, 1)
            gate_up(1, 1, True)
            down(0, 0)
            gate_up(1, 2, True)
            down(0, 1)
            gate_up(1, 3, True)
            with pe.Fori(2, E - 1) as e:
                expert(e, False, False)
            expert(E - 1, False, True)
            down(E - 1, 0)
            down(E - 1, 1)


_INS = ["L0_attn_x", "L0_attn_wq", "L0_attn_wk", "L0_attn_wv", "L0_attn_wo", "L0_ffn_router_weight", "L0_ffn_router_bias",
        "L0_ffn_gate_up_proj", "L0_ffn_gate_up_proj_bias", "L0_ffn_down_proj", "L0_ffn_down_proj_bias"]


def _tables():
    half = D // 2
    freqs = np.power(np.float32(10000.0), -np.arange(half, dtype=np.float32) / np.float32(half)).astype(np.float32)
    rad = (freqs[:, None] * np.arange(T, dtype=np.float32)[None, :]).astype(np.float32)
    cos, sin = np.cos(rad).astype(np.float32), np.sin(rad).astype(np.float32)
    mask = np.zeros((P, T), np.float32)
    mask[:, P:] = np.where(np.arange(P)[None, :] > np.arange(P)[:, None], np.float32(NEG), np.float32(0.0))
    return {
        "rope_cos": np.concatenate([cos, cos], 0),
        "rope_sin": np.concatenate([-sin, sin], 0),
        "causal_mask": mask,
        "identity": np.eye(P, dtype=np.float32),
    }


def kernel(**inputs):
    import concourse.bacc as bacc
    from concourse.bass_utils import run_bass_kernel_spmd

    nc = bacc.Bacc("TRN2", target_bir_lowering=False, num_devices=1)
    arrays, args = {}, []
    given = {name: np.ascontiguousarray(inputs[name]) for name in _INS}
    for name, a in {**given, **_tables()}.items():
        arrays[f"in_{name}_dram"] = a
        args.append(nc.dram_tensor(f"in_{name}_dram", a.shape, mybir.dt.from_np(a.dtype), kind="ExternalInput").ap())
    args.append(nc.dram_tensor("out_0_dram", (B, T, M), F32, kind="ExternalOutput").ap())
    block_kernel(nc, *args)
    r = run_bass_kernel_spmd(nc, [arrays], core_ids=[0])
    return r.results[0]["out_0_dram"]
```

```python
from contextlib import ExitStack

import numpy as np

import concourse.bass as bass
from concourse import mybir

F32 = mybir.dt.float32
F32R = mybir.dt.float32r
ALU = mybir.AluOpType
ACT = mybir.ActivationFunctionType
AX_X = mybir.AxisListType.X

P = 128
B, T, M = 4, 256, 256
H, D = 16, 128
E, DF, TOP = 16, 256, 4
N = B * T
KM = M // P
TILES = N // P
HALF = N // 2
GROUPS = H // 2
PAIRS = 2 * B
QK_CHUNKS = 8
LEAD = 4
EPS = 1e-5
NEG = -1e30
ALPHA, LIMIT = 1.702, 7.0
SENTINEL = -3.0e38
FILL = 3.0e38


def pair_head(p):
    return (p // 2) % 2


def pair_batch(p):
    return 2 * (p // 4) + p % 2


def block_kernel(nc, x_d, wq_d, wk_d, wv_d, wo_d, rw_d, rb_d, gu_d, gub_d, dn_d, dnb_d,
                 rope_cos_d, rope_sin_d, mask_d, ident_d, out_d):
    ctx = ExitStack()
    with ctx:
        def sb(name, shape, dt=F32):
            return ctx.enter_context(nc.sbuf_tensor(name, shape, dt))

        def sem(name):
            return ctx.enter_context(nc.semaphore(name))

        x = sb("x", [P, TILES, M])
        xn = sb("xn", [P, TILES, M])
        xT_h = sb("xT_h", [P, KM, N], F32R)
        xT_l = sb("xT_l", [P, KM, N], F32R)
        attn = sb("attn", [P, TILES, M])
        moe = sb("moe", [P, TILES, M])
        rope_cos = sb("rope_cos", [P, T])
        rope_sin = sb("rope_sin", [P, T])
        mask = sb("mask", [P, T])
        ident = sb("ident", [P, P])
        stats = sb("stats", [P, TILES, 6])
        mean_var = sb("mean_var", [P, TILES, 2])
        var_eps = sb("var_eps", [P, TILES])
        minus_mean = sb("minus_mean", [P, TILES])
        rstd = sb("rstd", [P, TILES])
        shift = sb("shift", [P, TILES])
        minus_half = sb("minus_half", [P, TILES])

        raw_qk = [sb(f"raw_qk{a}", [P, 2, KM, D]) for a in range(2)]
        qk_h = [sb(f"qk_h{a}", [P, 2, KM, D], F32R) for a in range(2)]
        qk_l = [sb(f"qk_l{a}", [P, 2, KM, D], F32R) for a in range(2)]
        raw_v = sb("raw_v", [P, KM, 2 * D])
        wv_h = sb("wv_h", [P, KM, 2 * D], F32R)
        wv_l = sb("wv_l", [P, KM, 2 * D], F32R)
        raw_o = [sb(f"raw_o{a}", [P, M]) for a in range(2)]
        wo_h = [sb(f"wo_h{a}", [P, M], F32R) for a in range(2)]
        wo_l = [sb(f"wo_l{a}", [P, M], F32R) for a in range(2)]
        qkT = sb("qkT", [P, 2, 4, HALF])
        V = sb("V", [P, B, 2, 2 * D])
        by_cos = sb("by_cos", [P, 2, HALF])
        by_sin = sb("by_sin", [P, 2, HALF])
        score = sb("score", [P, 2, P + T])
        row_bias = sb("row_bias", [P, 2, 2])
        row_sum = sb("row_sum", [P, 2, 2])
        row_rec = sb("row_rec", [P, 2, 2])
        prob = sb("prob", [P, 2, P + T])
        probT = sb("probT", [P, P + T])
        oT_h = sb("oT_h", [P, 2, T], F32R)
        oT_l = sb("oT_l", [P, 2, T], F32R)

        raw_gu = sb("raw_gu", [P, KM, 2 * DF])
        gu_h = [sb(f"gu_h{r}", [P, KM, 2, P], F32R) for r in range(2)]
        gu_l = [sb(f"gu_l{r}", [P, KM, 2, P], F32R) for r in range(2)]
        raw_dn = sb("raw_dn", [P, 2, M])
        dn_h = sb("dn_h", [P, 2, M], F32R)
        dn_l = sb("dn_l", [P, 2, M], F32R)
        gub_rows = sb("gub_rows", [2 * E, 2 * P])
        gate_bias = sb("gate_bias", [P, 2 * E])
        up_bias = sb("up_bias", [P, 2 * E])
        dnb = sb("dnb", [E, M])
        gate = sb("gate", [P, 2, HALF])
        glu = sb("glu", [P, 2, HALF])
        up = sb("up", [P, 2, HALF])
        act = sb("act", [P, 2, HALF])
        actT_h = sb("actT_h", [P, 2, N], F32R)
        actT_l = sb("actT_l", [P, 2, N], F32R)

        rw = sb("rw", [E, M])
        rwT_h = sb("rwT_h", [P, KM, E], F32R)
        rwT_l = sb("rwT_l", [P, KM, E], F32R)
        rb = sb("rb", [E, 1])
        logitsT = sb("logitsT", [E, N])
        logits = sb("logits", [P, TILES, E + 8])
        best = sb("best", [P, TILES, 8])
        marked = sb("marked", [P, TILES, E + 8])
        chosen = sb("chosen", [P, TILES, E])
        shifted = sb("shifted", [P, TILES, E])
        expo = sb("expo", [P, TILES, E])
        weight = sb("weight", [P, TILES, E])
        wsum = sb("wsum", [P, TILES])
        wrec = sb("wrec", [P, TILES])
        route = sb("route", [P, TILES, E])
        routeT = sb("routeT", [E, N])

        bank = [ctx.enter_context(nc.psum_tensor(f"bank{i}", [P, 512], F32)) for i in range(8)]
        ps_qk = bank[0:2]
        ps_s, ps_pT, ps_oT, ps_v = bank[2:6]
        ps_r = bank[6:8]
        ps_gu = [bank[0:2], bank[2:4]]
        ps_dn = [bank[4:6], bank[6:8]]

        XT_BANKS = [bank[i] for i in (2, 3, 4, 6, 0, 1, 4, 5)]

        dma_x = [sem(f"dma_x{u}") for u in range(4)]
        dma_ident = sem("dma_ident")
        dma_rope = sem("dma_rope")
        dma_mask = sem("dma_mask")
        dma_small = sem("dma_small")
        dma_qk = [sem(f"dma_qk{a}") for a in range(2)]
        dma_v = sem("dma_v")
        dma_o = [sem(f"dma_o{a}") for a in range(2)]
        dma_gu = sem("dma_gu")
        dma_dn = sem("dma_dn")
        dma_out = sem("dma_out")

        pool_const = sem("pool_const")
        pool_rstd = sem("pool_rstd")
        pool_shift = sem("pool_shift")
        pool_sin = sem("pool_sin")
        pool_qk = [sem(f"pool_qk{a}") for a in range(2)]
        pool_v = sem("pool_v")
        pool_o = [sem(f"pool_o{a}") for a in range(2)]
        pool_gu = [sem(f"pool_gu{r}") for r in range(2)]
        pool_dn = sem("pool_dn")
        pool_act = sem("pool_act")

        act_norm = sem("act_norm")
        act_xT = sem("act_xT")
        act_logits = sem("act_logits")
        act_swap = sem("act_swap")
        act_exp = sem("act_exp")
        act_pT = sem("act_pT")
        act_v = sem("act_v")
        act_oT = sem("act_oT")
        act_qk = [sem(f"act_qk{a}") for a in range(2)]
        act_wv = sem("act_wv")
        act_wo = [sem(f"act_wo{a}") for a in range(2)]
        act_gu = [sem(f"act_gu{r}") for r in range(2)]
        act_dn = sem("act_dn")
        act_glu = sem("act_glu")
        act_act = sem("act_act")
        act_small = sem("act_small")

        dve_stat = sem("dve_stat")
        dve_var = sem("dve_var")
        dve_xT = sem("dve_xT")
        dve_cos = sem("dve_cos")
        dve_rope = sem("dve_rope")
        dve_max = sem("dve_max")
        dve_rec = sem("dve_rec")
        dve_norm = sem("dve_norm")
        dve_oT = sem("dve_oT")
        dve_attn = sem("dve_attn")
        dve_small = sem("dve_small")
        dve_route = sem("dve_route")
        dve_routeT = sem("dve_routeT")
        dve_gate = sem("dve_gate")
        dve_up = sem("dve_up")
        dve_act = sem("dve_act")
        dve_moe = sem("dve_moe")
        dve_out = sem("dve_out")

        pe_xT = sem("pe_xT")
        pe_qk = sem("pe_qk")
        pe_s = sem("pe_s")
        pe_pT = sem("pe_pT")
        pe_oT = sem("pe_oT")
        pe_v = sem("pe_v")
        pe_r = sem("pe_r")
        pe_small = sem("pe_small")
        pe_logitsT = sem("pe_logitsT")
        pe_logits = sem("pe_logits")
        pe_routeT = sem("pe_routeT")
        pe_dnb = sem("pe_dnb")
        pe_gu = sem("pe_gu")
        pe_dn = sem("pe_dn")

        def step_rc(e, q):
            return (q % 2, q // 2) if isinstance(e, int) and e == 0 else (q // 2, q % 2)

        NORMS = ([("x", u) for u in range(4)] + [("a", 0), ("a", 1), ("b", 0), ("b", 1), ("a", 2), ("a", 3), ("b", 2), ("b", 3)]
                 + [("moe", u) for u in range(4)])
        V_CHUNK = {2: (0, 2), 3: (0, 3), 6: (1, 0), 7: (1, 1)}

        x_rows = x_d.rearrange("b (s p) m -> p (b s) m", p=P)
        out_rows = out_d.rearrange("b (s p) m -> p (b s) m", p=P)
        wq_cols = wq_d.rearrange("(k p) h d -> h p k d", p=P)
        wk_cols = wk_d.rearrange("(k p) h d -> h p k d", p=P)
        wv_cols = wv_d.rearrange("(k p) (g a) d -> g p k (a d)", p=P, a=2)
        gu_rows = gu_d.rearrange("e (k p) c -> e p k c", p=P)
        dn_rows = dn_d.rearrange("e (k p) m -> e p k m", p=P)

        block = ctx.enter_context(nc.Block())

        @block.sync
        def _(sp):
            def load_x(u):
                sp.dma_start(x[:, 2 * u:2 * u + 2, :], x_rows[:, 2 * u:2 * u + 2, :]).then_inc(dma_x[u], 16)

            def load_qk(a, g):
                sp.dma_start(raw_qk[a][:, 0, :, :], wq_cols[2 * g + a]).then_inc(dma_qk[a], 16)
                sp.dma_start(raw_qk[a][:, 1, :, :], wk_cols[2 * g + a]).then_inc(dma_qk[a], 16)

            def load_v(g):
                sp.dma_start(raw_v[:, :, :], wv_cols[g]).then_inc(dma_v, 16)

            def load_o(a, g):
                sp.dma_start(raw_o[a][:, :], wo_d[2 * g + a]).then_inc(dma_o[a], 16)

            load_x(0)
            load_x(1)
            load_qk(0, 0)
            sp.dma_start(ident[:, :], ident_d).then_inc(dma_ident, 16)
            load_x(2)
            sp.dma_start(rope_cos[:, :], rope_cos_d).then_inc(dma_rope, 16)
            sp.dma_start(rope_sin[:, :], rope_sin_d).then_inc(dma_rope, 16)
            load_qk(1, 0)
            load_x(3)
            load_v(0)
            sp.dma_start(mask[:, :], mask_d).then_inc(dma_mask, 16)
            load_o(0, 0)
            load_o(1, 0)
            sp.dma_start(rw[:, :], rw_d).then_inc(dma_small, 16)
            sp.dma_start(rb[:, :], rb_d.rearrange("(e o) -> e o", o=1)).then_inc(dma_small, 16)
            sp.dma_start(gub_rows[:, :], gub_d.rearrange("e (r c) -> (e r) c", r=2)).then_inc(dma_small, 16)
            sp.dma_start(dnb[:, :], dnb_d).then_inc(dma_small, 16)
            with sp.Fori(1, GROUPS) as g:
                sp.wait_ge(pool_qk[0], g)
                load_qk(0, g)
                sp.wait_ge(pool_qk[1], g)
                load_qk(1, g)
                sp.wait_ge(pool_v, g)
                load_v(g)
                sp.wait_ge(pool_o[0], g)
                load_o(0, g)
                sp.wait_ge(pool_o[1], g)
                load_o(1, g)
            sp.dma_start(raw_gu[:, :, :], gu_rows[0]).then_inc(dma_gu, 16)
            sp.dma_start(raw_dn[:, :, :], dn_rows[0]).then_inc(dma_dn, 16)
            with sp.Fori(1, E) as e:
                sp.wait_ge(pool_gu[0], e)
                sp.wait_ge(pool_gu[1], e)
                sp.dma_start(raw_gu[:, :, :], gu_rows[e]).then_inc(dma_gu, 16)
                sp.wait_ge(pool_dn, e)
                sp.dma_start(raw_dn[:, :, :], dn_rows[e]).then_inc(dma_dn, 16)
            for u in range(4):
                sp.wait_ge(dve_out, u + 1)
                sp.dma_start(out_rows[:, 2 * u:2 * u + 2, :], xn[:, 2 * u:2 * u + 2, :]).then_inc(dma_out, 16)
            sp.wait_ge(dma_out, 16 * 4)

        @block.gpsimd
        def _(pool):
            pool.memset(minus_half[:, :], -0.5).then_inc(pool_const, 1)
            pool.memset(attn[:, :, :], 0.0).then_inc(pool_const, 1)
            pool.memset(logits[:, :, E:E + 8], SENTINEL).then_inc(pool_const, 1)
            pool.wait_ge(pool_const, 1)

            def power(kind, u):
                n = NORMS.index((kind, u))
                tiles = slice(2 * u, 2 * u + 2)
                pool.wait_ge(dve_var, n + 1)
                pool.tensor_tensor(rstd[:, tiles], var_eps[:, tiles], minus_half[:, tiles], ALU.pow).then_inc(pool_rstd, 1)
                pool.wait_ge(pool_rstd, n + 1)
                pool.tensor_tensor(shift[:, tiles], minus_mean[:, tiles], rstd[:, tiles], ALU.mult).then_inc(pool_shift, 1)

            def low(out, raw, high, ready, n, done):
                pool.wait_ge(ready, n)
                pool.tensor_tensor(out, raw, high.bitcast(F32), ALU.subtract).then_inc(done, 1)

            def low_qk(a, g):
                low(qk_l[a][:, :, :, :], raw_qk[a][:, :, :, :], qk_h[a][:, :, :, :], act_qk[a], g + 1, pool_qk[a])

            def low_v(g):
                low(wv_l[:, :, :], raw_v[:, :, :], wv_h[:, :, :], act_wv, g + 1, pool_v)

            def low_o(a, g):
                low(wo_l[a][:, :], raw_o[a][:, :], wo_h[a][:, :], act_wo[a], g + 1, pool_o[a])

            def times_sine(n, w):
                pool.wait_ge(act_swap, n + 1)
                v = by_sin[:, w, :].rearrange("p (b t) -> p b t", b=2)
                pool.tensor_tensor(v, v, rope_sin[:, :].unsqueeze(1).broadcast_to([P, 2, T]), ALU.mult).then_inc(pool_sin, 1)

            def slot(g, p, last):
                if not (last and p >= QK_CHUNKS - LEAD):
                    times_sine(QK_CHUNKS * g + p + LEAD, p % 2)
                if p == 1:
                    low_o(1, g)
                if not last:
                    if p == 2:
                        low_qk(0, g + 1)
                    if p == 4:
                        low_qk(1, g + 1)
                    if p == 5:
                        low_v(g + 1)
                    if p == 7:
                        low_o(0, g + 1)

            power("x", 0)
            power("x", 1)
            low_qk(0, 0)
            power("x", 2)
            low_qk(1, 0)
            power("x", 3)
            pool.wait_ge(dma_rope, 32)
            for n in range(LEAD):
                times_sine(n, n % 2)
                if n == 1:
                    low_v(0)
            low_o(0, 0)
            with pool.Fori(0, GROUPS - 1) as g:
                for p in range(PAIRS):
                    slot(g, p, False)
            for p in range(PAIRS):
                slot(GROUPS - 1, p, True)

            def gu_view(r):
                return raw_gu[:, :, :].rearrange("p k (d s) -> p k s d", s=2)[:, :, :, r * P:(r + 1) * P]

            def low_gu(r, e):
                low(gu_l[r][:, :, :, :], gu_view(r), gu_h[r][:, :, :, :], act_gu[r], e + 1, pool_gu[r])

            def low_dn(e):
                low(dn_l[:, :, :], raw_dn[:, :, :], dn_h[:, :, :], act_dn, e + 1, pool_dn)

            for kind, u in NORMS[4:12]:
                power(kind, u)
                if (kind, u) == ("b", 1):
                    low_gu(0, 0)
                if (kind, u) == ("a", 3):
                    low_gu(1, 0)
            low_dn(0)

            def low_act(e, q):
                r, c = step_rc(e, q)
                pool.wait_ge(act_act, 4 * e + q + 1)
                pool.tensor_tensor(actT_l[:, r, c * HALF:(c + 1) * HALF], act[:, q % 2, :],
                                   actT_h[:, r, c * HALF:(c + 1) * HALF].bitcast(F32),
                                   ALU.subtract).then_inc(pool_act, 1)

            def expert(e, last):
                low_gu(1, e)
                if not last:
                    low_gu(0, e + 1)
                low_act(e, 0)
                low_act(e, 1)
                low_dn(e)
                low_act(e, 2)
                low_act(e, 3)

            for q in range(4):
                if q == 2:
                    low_gu(0, 1)
                low_act(0, q)
            with pool.Fori(1, E - 1) as e:
                expert(e, False)
            expert(E - 1, True)
            for u in range(4):
                power("moe", u)

        @block.scalar
        def _(sc):
            def copy(out, in_):
                return sc.activation(out, in_, ACT.Copy)

            def high_qk(a, g, free=True):
                sc.wait_ge(dma_qk[a], 32 * g + 32)
                if free:
                    sc.wait_ge(pe_qk, QK_CHUNKS * g - 2 + 2 * a)
                copy(qk_h[a][:, :, :, :], raw_qk[a][:, :, :, :]).then_inc(act_qk[a], 1)

            def high_v(g, free=True):
                sc.wait_ge(dma_v, 16 * g + 16)
                if free:
                    sc.wait_ge(pe_v, 4 * g)
                copy(wv_h[:, :, :], raw_v[:, :, :]).then_inc(act_wv, 1)

            def high_o(a, g, free=True):
                sc.wait_ge(dma_o[a], 16 * g + 16)
                if free:
                    sc.wait_ge(pe_r, PAIRS * g - (0 if a else 2))
                copy(wo_h[a][:, :], raw_o[a][:, :]).then_inc(act_wo[a], 1)

            def swap(n, w):
                sc.wait_ge(dve_cos, n + 1)
                sc.wait_ge(dve_rope, n - 1) if not (isinstance(n, int) and n < 2) else None
                copy(by_sin[0:64, w, :], ps_qk[w][64:128, :])
                copy(by_sin[64:128, w, :], ps_qk[w][0:64, :]).then_inc(act_swap, 1)

            def softmax_exp(g, p):
                k = PAIRS * g + p
                sc.wait_ge(dve_max, k + 1)
                if not (isinstance(k, int) and k < 2):
                    sc.wait_ge(pe_pT, k - 1)
                for i, (lo, hi) in enumerate([(0, P), (P, P + T)]):
                    e = sc.activation(prob[:, p % 2, lo:hi], score[:, p % 2, lo:hi], ACT.Exp,
                                      bias=row_bias[:, p % 2, i:i + 1], scale=-1.0,
                                      accum_out=row_sum[:, p % 2, i:i + 1])
                e.then_inc(act_exp, 1)

            def values(m, b, free):
                sc.wait_ge(pe_v, m + 1)
                if free is not None:
                    sc.wait_ge(pe_oT, free)
                copy(V[:, b, :, :], ps_v[:, :].rearrange("p (s c) -> p s c", s=2)).then_inc(act_v, 1)

            def oT_high(g, p):
                k = PAIRS * g + p
                sc.wait_ge(pe_oT, k + 1)
                if not (isinstance(k, int) and k < 2):
                    sc.wait_ge(pe_r, k - 1)
                copy(oT_h[:, p % 2, :], ps_oT[:, 0:T]).then_inc(act_oT, 1)

            def slot(g, p, first, last):
                if not (first and p == 0):
                    oT_high(g - (p == 0), (p - 1) % PAIRS)
                if not (last and p == PAIRS - 1):
                    softmax_exp(g + (p == PAIRS - 1), (p + 1) % PAIRS)
                sc.wait_ge(pe_pT, PAIRS * g + p + 1)
                copy(probT[:, :], ps_pT[:, 0:P + T]).then_inc(act_pT, 1)
                if not (last and p >= QK_CHUNKS - LEAD):
                    swap(QK_CHUNKS * g + p + LEAD, p % 2)
                if p in V_CHUNK and not (last and V_CHUNK[p][0]):
                    dg, b = V_CHUNK[p]
                    free = None if first and not dg else PAIRS * (g + dg - 1) + 4 * (b // 2) + 2 + b % 2 + 1
                    values(4 * (g + dg) + b, b, free)
                if p == 1:
                    high_o(1, g, not first)
                if not last:
                    if p == 2:
                        high_qk(0, g + 1)
                    if p == 4:
                        high_qk(1, g + 1)
                    if p == 5:
                        high_v(g + 1)
                    if p == 7:
                        high_o(0, g + 1)

            def normalise(kind, u, out, src):
                sc.wait_ge(pool_shift, NORMS.index((kind, u)) + 1)
                for t in (2 * u, 2 * u + 1):
                    m = sc.activation(out[:, t, :], src[:, t, :], ACT.Identity, bias=shift[:, t:t + 1], scale=rstd[:, t:t + 1])
                m.then_inc(act_norm, 1)

            def xT_high(n, bank_of):
                sc.wait_ge(pe_xT, n + 1)
                c = (n % 4) * T
                copy(xT_h[:, :, c:c + T], bank_of[:, :].rearrange("p (k t) -> p k t", k=KM)).then_inc(act_xT, 1)

            normalise("x", 0, xn, x)
            high_qk(0, 0, False)
            normalise("x", 1, xn, x)
            xT_high(0, XT_BANKS[0])
            xT_high(1, XT_BANKS[1])
            high_qk(1, 0, False)
            normalise("x", 2, xn, x)
            swap(0, 0)
            normalise("x", 3, xn, x)
            swap(1, 1)
            high_v(0, False)
            xT_high(2, XT_BANKS[2])
            swap(2, 0)
            xT_high(3, XT_BANKS[3])
            swap(3, 1)
            high_o(0, 0, False)
            values(0, 0, None)
            softmax_exp(0, 0)
            values(1, 1, None)
            for p in range(PAIRS):
                slot(0, p, True, False)
            with sc.Fori(1, GROUPS - 1) as g:
                for p in range(PAIRS):
                    slot(g, p, False, False)
            for p in range(PAIRS):
                slot(GROUPS - 1, p, False, True)
                if p >= 6:
                    normalise("a", p - 6, attn, attn)
            oT_high(GROUPS - 1, PAIRS - 1)

            def gu_view(r):
                return raw_gu[:, :, :].rearrange("p k (d s) -> p k s d", s=2)[:, :, :, r * P:(r + 1) * P]

            def high_gu(r, e, free=True):
                sc.wait_ge(dma_gu, 16 * e + 16)
                if free:
                    sc.wait_ge(pe_gu, 3 if isinstance(e, int) and e == 1 and r == 0 else 4 * e - 2 + 2 * r)
                for k in range(KM):
                    c = copy(gu_h[r][:, k, :, :], gu_view(r)[:, k, :, :])
                c.then_inc(act_gu[r], 1)

            def high_dn(e, free=True):
                sc.wait_ge(dma_dn, 16 * e + 16)
                if free:
                    sc.wait_ge(pe_dn, 4 * e)
                copy(dn_h[:, :, :], raw_dn[:, :, :]).then_inc(act_dn, 1)

            def gelu(e, q, first):
                s = 4 * e + q
                sc.wait_ge(dve_gate, s + 1)
                if not (first and q < 2):
                    sc.wait_ge(dve_act, s - 1)
                sc.activation(glu[:, q % 2, :], gate[:, q % 2, :], ACT.Gelu_apprx_sigmoid).then_inc(act_glu, 1)

            def act_high(e, q, first):
                s = 4 * e + q
                r, c = step_rc(e, q)
                sc.wait_ge(dve_act, s + 1)
                if not first:
                    sc.wait_ge(pe_dn, 4 * (e - 1) + 2 * c + 2)
                copy(actT_h[:, r, c * HALF:(c + 1) * HALF], act[:, q % 2, :]).then_inc(act_act, 1)

            def expert(e, last):
                high_gu(1, e)
                gelu(e, 0, False)
                gelu(e, 1, False)
                if not last:
                    high_gu(0, e + 1)
                act_high(e, 0, False)
                gelu(e, 2, False)
                act_high(e, 1, False)
                high_dn(e)
                act_high(e, 2, False)
                gelu(e, 3, False)
                act_high(e, 3, False)

            high_gu(0, 0, False)
            normalise("b", 0, xn, x)
            normalise("b", 1, xn, x)
            xT_high(4, XT_BANKS[4])
            xT_high(5, XT_BANKS[5])
            normalise("a", 2, attn, attn)
            normalise("a", 3, attn, attn)
            high_gu(1, 0, False)
            normalise("b", 2, xn, x)
            normalise("b", 3, xn, x)
            high_dn(0, False)
            gelu(0, 0, True)
            xT_high(6, XT_BANKS[6])
            xT_high(7, XT_BANKS[7])
            act_high(0, 0, True)
            gelu(0, 1, True)
            act_high(0, 1, True)
            for c in range(2):
                sc.wait_ge(pe_logitsT, c + 1)
                sc.activation(logitsT[:, c * HALF:(c + 1) * HALF], bank[6 + c][0:E, :], ACT.Identity,
                              bias=rb[:, 0:1]).then_inc(act_logits, 1)
            high_gu(0, 1)
            gelu(0, 2, True)
            sc.wait_ge(dve_small, 8)
            sc.activation(expo[:, :, :], shifted[:, :, :], ACT.Exp).then_inc(act_small, 1)
            act_high(0, 2, True)
            gelu(0, 3, True)
            act_high(0, 3, True)
            with sc.Fori(1, E - 1) as e:
                expert(e, False)
            expert(E - 1, True)
            for u in range(4):
                normalise("moe", u, moe, moe)

        @block.vector
        def _(dve):
            steps = [0]

            def chain(ins):
                steps[0] += 1
                ins.then_inc(dve_stat, 1)
                dve.wait_ge(dve_stat, steps[0])

            def row_stats(src, u):
                tiles = slice(2 * u, 2 * u + 2)
                for t in (2 * u, 2 * u + 1):
                    s = dve.bn_stats(stats[:, t, :], src[:, t, :])
                chain(s)
                for t in (2 * u, 2 * u + 1):
                    s = dve.bn_aggr(mean_var[:, t, :], stats[:, t, :])
                chain(s)
                dve.tensor_scalar(minus_mean[:, tiles], mean_var[:, tiles, 0], -1.0, None, ALU.mult)
                dve.tensor_scalar(var_eps[:, tiles], mean_var[:, tiles, 1], EPS, None, ALU.add).then_inc(dve_var, 1)

            def xT_low(n):
                dve.wait_ge(act_xT, n + 1)
                c = (n % 4) * T
                dve.tensor_tensor(xT_l[:, :, c:c + T], XT_BANKS[n][:, :].rearrange("p (k t) -> p k t", k=KM),
                                  xT_h[:, :, c:c + T].bitcast(F32), ALU.subtract).then_inc(dve_xT, 1)

            for u in range(4):
                dve.wait_ge(dma_x[u], 16)
                row_stats(x, u)
                if u == 2:
                    xT_low(0)
                    xT_low(1)

            def cosine(n, w):
                dve.wait_ge(pe_qk, n + 1)
                if not (isinstance(n, int) and n < 2):
                    dve.wait_ge(dve_rope, n - 1)
                v = by_cos[:, w, :].rearrange("p (b t) -> p b t", b=2)
                dve.tensor_tensor(v, ps_qk[w][:, :].rearrange("p (b t) -> p b t", b=2),
                                  rope_cos[:, :].unsqueeze(1).broadcast_to([P, 2, T]), ALU.mult).then_inc(dve_cos, 1)

            def rotate(n, w, j, free):
                dve.wait_ge(pool_sin, n + 1)
                dve.wait_ge(dve_cos, n + 1)
                if free is not None:
                    dve.wait_ge(pe_s, free)
                dve.tensor_tensor(qkT[:, w, j, :], by_cos[:, w, :], by_sin[:, w, :], ALU.add).then_inc(dve_rope, 1)

            def await_scores(g, p):
                k = PAIRS * g + p
                dve.wait_ge(pe_s, k + 1)
                if not (isinstance(k, int) and k < 2):
                    dve.wait_ge(act_exp, k - 1)
                dve.memset(row_sum[:, p % 2, :], 0.0)

            def row_max(p):
                for i, (lo, hi) in enumerate([(0, P), (P, P + T)]):
                    m = dve.tensor_tensor_reduce(score[:, p % 2, lo:hi], ps_s[:, lo:hi], mask[:, P:T] if i == 0 else mask[:, :],
                                                 -1.0 / D, FILL, ALU.add, ALU.min, row_bias[:, p % 2, i:i + 1])
                m.then_inc(dve_max, 1)

            def normalise_prob(g, p):
                k = PAIRS * g + p
                dve.wait_ge(act_exp, k + 1)
                dve.reciprocal(row_rec[:, p % 2, :], row_sum[:, p % 2, :]).then_inc(dve_rec, 1)
                dve.wait_ge(dve_rec, k + 1)
                for i, (lo, hi) in enumerate([(0, P), (P, P + T)]):
                    m = dve.tensor_scalar(prob[:, p % 2, lo:hi], prob[:, p % 2, lo:hi], row_rec[:, p % 2, i:i + 1],
                                          None, ALU.mult)
                m.then_inc(dve_norm, 1)

            def oT_low(g, p):
                dve.wait_ge(act_oT, PAIRS * g + p + 1)
                dve.tensor_tensor(oT_l[:, p % 2, :], ps_oT[:, 0:T], oT_h[:, p % 2, :].bitcast(F32),
                                  ALU.subtract).then_inc(dve_oT, 1)

            def add_attn(g, p):
                dve.wait_ge(pe_r, PAIRS * g + p + 1)
                b = pair_batch(p)
                v = attn[:, 2 * b:2 * b + 2, :]
                dve.tensor_tensor(v, ps_r[b % 2][:, :].rearrange("p (s m) -> p s m", s=2), v, ALU.add).then_inc(dve_attn, 1)

            def slot(g, p, first, last, meanwhile=lambda: None):
                if not (last and p == PAIRS - 1):
                    await_scores(g + (p == PAIRS - 1), (p + 1) % PAIRS)
                    row_max((p + 1) % PAIRS)
                if not (first and p == 0):
                    oT_low(g - (p == 0), (p - 1) % PAIRS)
                if not (last and p > QK_CHUNKS - LEAD):
                    n, unit = QK_CHUNKS * g + p + LEAD - 1, (p + LEAD - 1) // 2
                    free = None if first and unit < 4 else PAIRS * g + 2 * unit - 6
                    rotate(n, (p + 1) % 2, unit % 4, free)
                meanwhile()
                if not (last and p >= QK_CHUNKS - LEAD):
                    cosine(QK_CHUNKS * g + p + LEAD, p % 2)
                if not (last and p == PAIRS - 1):
                    normalise_prob(g + (p == PAIRS - 1), (p + 1) % PAIRS)
                if not (first and p < 2) and pair_head((p - 2) % PAIRS):
                    add_attn(g - (p < 2), (p - 2) % PAIRS)

            dve.wait_ge(dma_rope, 32)
            for n in range(LEAD):
                cosine(n, n % 2)
                if n >= 1:
                    rotate(n - 1, (n - 1) % 2, (n - 1) // 2, None)
            xT_low(2)
            xT_low(3)
            await_scores(0, 0)
            dve.wait_ge(dma_mask, 16)
            row_max(0)
            normalise_prob(0, 0)
            dve.wait_ge(pool_const, 3)
            for p in range(PAIRS):
                slot(0, p, True, False)
            with dve.Fori(1, GROUPS - 1) as g:
                for p in range(PAIRS):
                    slot(g, p, False, False)
            def attn_stats(u):
                dve.wait_ge(dve_attn, 4 * (GROUPS - 1) + u + 1)
                row_stats(attn, u)

            def residual(u):
                dve.wait_ge(act_norm, NORMS.index(("a", u)) + 1)
                v = x[:, 2 * u:2 * u + 2, :]
                chain(dve.tensor_tensor(v, attn[:, 2 * u:2 * u + 2, :], v, ALU.add))
                row_stats(x, u)

            def small_tables():
                dve.wait_ge(pe_small, 1)
                dve.tensor_copy(gate_bias[:, :], ps_v[:, 0:2 * E])
                dve.tensor_scalar(up_bias[:, :], ps_v[:, 2 * E:4 * E], 1.0, None, ALU.add)
                dve.tensor_copy(rwT_h[:, :, :], ps_v[:, 4 * E:6 * E].rearrange("p (k e) -> p k e", k=KM)).then_inc(dve_small, 1)
                dve.wait_ge(dve_small, 1)
                dve.tensor_tensor(rwT_l[:, :, :], ps_v[:, 4 * E:6 * E].rearrange("p (k e) -> p k e", k=KM),
                                  rwT_h[:, :, :].bitcast(F32), ALU.subtract).then_inc(dve_small, 1)

            meanwhile = {5: small_tables, 6: lambda: attn_stats(0), 7: lambda: attn_stats(1)}
            for p in range(PAIRS):
                slot(GROUPS - 1, p, False, True, meanwhile.get(p, lambda: None))
            residual(0)
            oT_low(GROUPS - 1, PAIRS - 1)
            residual(1)
            add_attn(GROUPS - 1, PAIRS - 2)
            attn_stats(2)
            add_attn(GROUPS - 1, PAIRS - 1)
            attn_stats(3)
            xT_low(4)
            xT_low(5)
            residual(2)
            residual(3)

            def router():
                dve.wait_ge(pe_logits, 1)
                dve.tensor_copy(logits[:, :, 0:E], bank[6][:, 0:TILES * E].rearrange("p (t e) -> p t e", e=E)).then_inc(dve_small, 1)
                dve.wait_ge(dve_small, 3)
                for t in range(TILES):
                    m = dve.max(best[:, t, :], logits[:, t, 0:E])
                m.then_inc(dve_small, 1)
                dve.wait_ge(dve_small, 4)
                dve.memset(best[:, :, TOP:8], SENTINEL).then_inc(dve_small, 1)
                dve.wait_ge(dve_small, 5)
                for t in range(TILES):
                    m = dve.match_replace(marked[:, t, :], best[:, t, :], logits[:, t, :], FILL)
                m.then_inc(dve_small, 1)
                dve.wait_ge(dve_small, 6)
                dve.tensor_tensor(chosen[:, :, :], marked[:, :, 0:E], logits[:, :, 0:E], ALU.not_equal).then_inc(dve_small, 1)
                dve.tensor_tensor(shifted[:, :, :], logits[:, :, 0:E], best[:, :, 0:1].broadcast_to([P, TILES, E]),
                                  ALU.subtract).then_inc(dve_small, 1)
                dve.wait_ge(act_small, 1)
                dve.wait_ge(dve_small, 8)
                dve.tensor_tensor(weight[:, :, :], expo[:, :, :], chosen[:, :, :], ALU.mult).then_inc(dve_small, 1)
                dve.wait_ge(dve_small, 9)
                dve.tensor_reduce(wsum[:, :], weight[:, :, :], AX_X, ALU.add).then_inc(dve_small, 1)
                dve.wait_ge(dve_small, 10)
                dve.reciprocal(wrec[:, :], wsum[:, :]).then_inc(dve_small, 1)
                dve.wait_ge(dve_small, 11)
                dve.tensor_tensor(route[:, :, :], weight[:, :, :], wrec[:, :].unsqueeze(2).broadcast_to([P, TILES, E]),
                                  ALU.mult).then_inc(dve_route, 1)
            def router_part_2():
                for c in range(2):
                    dve.wait_ge(pe_routeT, c + 1)
                    dve.tensor_copy(routeT[:, c * HALF:(c + 1) * HALF], bank[4 + c][0:E, :]).then_inc(dve_routeT, 1)
                for u in range(4):
                    dve.wait_ge(pe_dnb, u + 1)
                    dve.tensor_copy(moe[:, 2 * u:2 * u + 2, :], bank[4 + u][:, :].rearrange("p (s m) -> p s m", s=2)).then_inc(dve_moe, 1)
                dve.wait_ge(dve_moe, 4)

            def add_moe(e, c, batches=(0, 1)):
                for w in batches:
                    dve.wait_ge(pe_dn, 4 * e + 2 * c + w + 1)
                    if not (isinstance(e, int) and e == 0):
                        dve.wait_ge(dve_moe, 4 * e + 2 * c + w + 1)
                    for s in range(2):
                        t = 4 * c + 2 * w + s
                        m = dve.scalar_tensor_tensor(out=moe[:, t, :], in0=ps_dn[c][w][:, s * M:(s + 1) * M],
                                                     scalar=route[:, t, bass.ds(e, 1)], in1=moe[:, t, :],
                                                     op0=ALU.mult, op1=ALU.add)
                    m.then_inc(dve_moe, 1)

            def clamp(e, q, first):
                s = 4 * e + q
                r, _ = step_rc(e, q)
                dve.wait_ge(pe_gu, s + 1)
                if not (first and q < 2):
                    dve.wait_ge(act_glu, s - 1)
                dve.tensor_scalar(gate[:, q % 2, :], ps_gu[q % 2][0][:, :], gate_bias[:, bass.ds(2 * e + r, 1)], LIMIT,
                                  ALU.add, ALU.min).then_inc(dve_gate, 1)
                if not (first and q < 2):
                    dve.wait_ge(dve_act, s - 1)
                dve.tensor_scalar(up[:, q % 2, :], ps_gu[q % 2][1][:, :], up_bias[:, bass.ds(2 * e + r, 1)], 1.0 - LIMIT,
                                  ALU.add, ALU.max).then_inc(dve_up, 1)

            def gated(e, q, first):
                s = 4 * e + q
                dve.wait_ge(act_glu, s + 1)
                dve.wait_ge(dve_up, s + 1)
                if not (first and q < 2):
                    dve.wait_ge(pool_act, s - 1)
                dve.scalar_tensor_tensor(out=act[:, q % 2, :], in0=up[:, q % 2, :], scalar=1.0 + LIMIT,
                                         in1=glu[:, q % 2, :], op0=ALU.min, op1=ALU.mult).then_inc(dve_act, 1)

            def expert(e, first):
                for q in range(4):
                    clamp(e, q, first)
                    gated(e, q, first)
                    if q in (1, 2) and not first:
                        add_moe(e - 1, q - 1)

            clamp(0, 0, True)
            xT_low(6)
            xT_low(7)
            gated(0, 0, True)
            clamp(0, 1, True)
            gated(0, 1, True)
            clamp(0, 2, True)
            gated(0, 2, True)
            router()
            clamp(0, 3, True)
            gated(0, 3, True)
            clamp(1, 0, False)
            gated(1, 0, False)
            router_part_2()
            for q in range(1, 4):
                clamp(1, q, False)
                gated(1, q, False)
                if q < 3:
                    add_moe(0, q - 1)
            with dve.Fori(2, E) as e:
                expert(e, False)

            def finish(u):
                dve.wait_ge(act_norm, NORMS.index(("moe", u)) + 1)
                tiles = slice(2 * u, 2 * u + 2)
                dve.tensor_tensor(xn[:, tiles, :], moe[:, tiles, :], x[:, tiles, :], ALU.add).then_inc(dve_out, 1)

            for c in range(2):
                for w in range(2):
                    add_moe(E - 1, c, [w])
                    dve.wait_ge(dve_moe, 4 * E + 2 * c + w + 1)
                    row_stats(moe, 2 * c + w)
                finish(2 * c)
                finish(2 * c + 1)

        @block.tensor
        def _(pe):
            def product(out, pairs, first=True, last=True):
                terms = [t for lh, ll, rh, rl in pairs for t in ((lh, rh), (lh, rl), (ll, rh))]
                for i, (lhs, rhs) in enumerate(terms):
                    m = pe.matmul(out, lhs, rhs, start=first and i == 0, stop=last and i == len(terms) - 1,
                                  skip_group_check=not (first and last))
                return m

            def turn_rows(kind, u, n):
                pe.wait_ge(act_norm, NORMS.index((kind, u)) + 1)
                for s in range(2):
                    for k in range(KM):
                        m = pe.transpose(XT_BANKS[n][:, k * T + s * P:k * T + (s + 1) * P],
                                         xn[:, 2 * u + s, k * P:(k + 1) * P], ident[:, :])
                m.then_inc(pe_xT, 1)

            def qk_chunk(n, w, a, c, group, free):
                pe.wait_ge(pool_qk[a], group + 1)
                if free:
                    pe.wait_ge(act_swap, n - 1)
                cols = slice(c * HALF, (c + 1) * HALF)
                product(ps_qk[w][:, :], [(qk_h[a][:, w, k, :], qk_l[a][:, w, k, :], xT_h[:, k, cols], xT_l[:, k, cols])
                                         for k in range(KM)]).then_inc(pe_qk, 1)

            def v_chunk(m, b, group, free):
                pe.wait_ge(pool_v, group + 1)
                if free:
                    pe.wait_ge(act_v, m)
                for s in range(2):
                    cols = slice((2 * b + s) * P, (2 * b + s + 1) * P)
                    v = product(ps_v[:, s * T:(s + 1) * T], [(xT_h[:, k, cols], xT_l[:, k, cols], wv_h[:, k, :], wv_l[:, k, :])
                                                             for k in range(KM)])
                v.then_inc(pe_v, 1)

            def scores(g, p, free):
                j, o = p // 2, (p % 2) * T
                if p % 2 == 0:
                    pe.wait_ge(dve_rope, QK_CHUNKS * g + 2 * j + 2)
                if free:
                    pe.wait_ge(dve_max, PAIRS * g + p)
                pe.matmul(ps_s[:, 0:P], qkT[:, 0, j, o:o + P], qkT[:, 1, j, o:o + P], start=True, stop=True)
                pe.matmul(ps_s[:, P:P + T], qkT[:, 0, j, o + P:o + T], qkT[:, 1, j, o:o + T],
                          start=True, stop=True).then_inc(pe_s, 1)

            def turn_prob(g, p, free):
                pe.wait_ge(dve_norm, PAIRS * g + p + 1)
                if free:
                    pe.wait_ge(act_pT, PAIRS * g + p)
                for i in range(3):
                    m = pe.transpose(ps_pT[:, i * P:(i + 1) * P], prob[:, p % 2, i * P:(i + 1) * P], ident[:, :])
                m.then_inc(pe_pT, 1)

            def weigh_values(g, p, free):
                a, b = pair_head(p), pair_batch(p)
                pe.wait_ge(act_pT, PAIRS * g + p + 1)
                pe.wait_ge(act_v, 4 * g + b + 1)
                if free:
                    pe.wait_ge(dve_oT, PAIRS * g + p)
                pe.matmul(ps_oT[:, 0:T], V[:, b, 0, a * D:(a + 1) * D], probT[:, 0:T], start=True, stop=False,
                          skip_group_check=True)
                pe.matmul(ps_oT[:, P:T], V[:, b, 1, a * D:(a + 1) * D], probT[:, T:T + P], start=False, stop=True,
                          skip_group_check=True).then_inc(pe_oT, 1)

            def output_rows(g, p, first):
                a, b = pair_head(p), pair_batch(p)
                pe.wait_ge(dve_oT, PAIRS * g + p + 1)
                pe.wait_ge(pool_o[a], g + 1)
                if a == 0 and not (first and p < 2):
                    pe.wait_ge(dve_attn, 4 * g + 2 * (p // 4) + p % 2 - 1)
                for s in range(2):
                    m = product(ps_r[b % 2][:, s * M:(s + 1) * M],
                                [(oT_h[:, p % 2, s * P:(s + 1) * P], oT_l[:, p % 2, s * P:(s + 1) * P], wo_h[a][:, :], wo_l[a][:, :])],
                                first=(a == 0 and s == 0), last=(a == 1))
                m.then_inc(pe_r, 1)

            def slot(g, p, first, last):
                if not (last and p >= QK_CHUNKS - LEAD):
                    unit = (p + LEAD) // 2
                    qk_chunk(QK_CHUNKS * g + p + LEAD, p % 2, unit % 2, (unit // 2) % 2, g + (unit >= 4), True)
                turn_prob(g, p, not (first and p == 0))
                if not (first and p == 0):
                    output_rows(g - (p == 0), (p - 1) % PAIRS, first and p != 0)
                if not (last and p >= PAIRS - 2):
                    scores(g + (p >= PAIRS - 2), (p + 2) % PAIRS, True)
                if p in V_CHUNK and not (last and V_CHUNK[p][0]):
                    dg, b = V_CHUNK[p]
                    v_chunk(4 * (g + dg) + b, b, g + dg, True)
                weigh_values(g, p, not (first and p == 0))

            pe.wait_ge(dma_ident, 16)
            turn_rows("x", 0, 0)
            turn_rows("x", 1, 1)
            pe.wait_ge(dve_xT, 2)
            qk_chunk(0, 0, 0, 0, 0, False)
            qk_chunk(1, 1, 0, 0, 0, False)
            turn_rows("x", 2, 2)
            qk_chunk(2, 0, 1, 0, 0, True)
            turn_rows("x", 3, 3)
            qk_chunk(3, 1, 1, 0, 0, True)
            v_chunk(0, 0, 0, False)
            scores(0, 0, False)
            v_chunk(1, 1, 0, True)
            pe.wait_ge(dve_xT, 4)
            scores(0, 1, True)
            for p in range(PAIRS):
                slot(0, p, True, False)
            with pe.Fori(1, GROUPS - 1) as g:
                for p in range(PAIRS):
                    slot(g, p, False, False)
            for p in range(PAIRS):
                slot(GROUPS - 1, p, False, True)
                if p == 4:
                    pe.wait_ge(act_v, 4 * GROUPS)
                    pe.wait_ge(dma_small, 64)
                    for s in range(2):
                        rows = gub_rows[:, :].rearrange("q (d s) -> q s d", s=2)[:, s, :]
                        pe.transpose(ps_v[:, s * 2 * E:(s + 1) * 2 * E], rows, ident[0:2 * E, 0:2 * E])
                    for k in range(KM):
                        m = pe.transpose(ps_v[:, (4 + k) * E:(5 + k) * E], rw[:, k * P:(k + 1) * P], ident[0:E, 0:E])
                    m.then_inc(pe_small, 1)
            output_rows(GROUPS - 1, PAIRS - 1, False)

            def gate_up(e, q, free):
                r, c = step_rc(e, q)
                pe.wait_ge(pool_gu[r], e + 1)
                if free:
                    pe.wait_ge(dve_up, 4 * e + q - 1)
                cols = slice(c * HALF, (c + 1) * HALF)
                for w in range(2):
                    m = product(ps_gu[q % 2][w][:, :],
                                [(gu_h[r][:, k, w, :], gu_l[r][:, k, w, :], xT_h[:, k, cols], xT_l[:, k, cols])
                                 for k in range(KM)])
                m.then_inc(pe_gu, 1)

            def down(e, c):
                if c == 0:
                    pe.wait_ge(pool_dn, e + 1)
                pe.wait_ge(pool_act, 4 * e + 2 + c + 1)
                for w in range(2):
                    pe.wait_ge(dve_moe, 4 * e + 2 * c + w + 1)
                    for s in range(2):
                        t = 4 * c + 2 * w + s
                        cols = slice(t * P, (t + 1) * P)
                        m = product(ps_dn[c][w][:, s * M:(s + 1) * M],
                                    [(actT_h[:, r, cols], actT_l[:, r, cols], dn_h[:, r, :], dn_l[:, r, :]) for r in range(2)])
                    m.then_inc(pe_dn, 1)

            def expert(e, first, last):
                for q in range(4):
                    gate_up(e, q, not (first and q < 2))
                    if q in (1, 2) and not first:
                        down(e - 1, q - 1)

            turn_rows("b", 0, 4)
            turn_rows("b", 1, 5)
            pe.wait_ge(dve_xT, 6)
            gate_up(0, 0, False)
            gate_up(0, 1, False)
            pe.wait_ge(dve_small, 2)
            turn_rows("b", 2, 6)
            turn_rows("b", 3, 7)
            pe.wait_ge(dve_xT, 8)
            for c in range(2):
                cols = slice(c * HALF, (c + 1) * HALF)
                product(bank[6 + c][0:E, :], [(rwT_h[:, k, :], rwT_l[:, k, :], xT_h[:, k, cols], xT_l[:, k, cols])
                                              for k in range(KM)]).then_inc(pe_logitsT, 1)
            gate_up(0, 2, True)
            pe.wait_ge(act_logits, 2)
            for t in range(TILES):
                m = pe.transpose(bank[6][:, t * E:(t + 1) * E], logitsT[:, t * P:(t + 1) * P], ident[0:E, 0:E])
            m.then_inc(pe_logits, 1)
            gate_up(0, 3, True)
            pe.wait_ge(dve_route, 1)
            for t in range(TILES):
                m = pe.transpose(bank[4 + t // 4][0:E, (t % 4) * P:(t % 4 + 1) * P], route[:, t, :], ident[:, :])
                if t % 4 == 3:
                    m.then_inc(pe_routeT, 1)
            gate_up(1, 0, True)
            pe.wait_ge(dve_routeT, 2)
            for t in range(TILES):
                m = pe.matmul(bank[4 + t // 2][:, (t % 2) * M:(t % 2 + 1) * M], routeT[:, t * P:(t + 1) * P], dnb[:, :],
                              start=True, stop=True)
                if t % 2 == 1:
                    m.then_inc(pe_dnb, 1)
            gate_up(1, 1, True)
            down(0, 0)
            gate_up(1, 2, True)
            down(0, 1)
            gate_up(1, 3, True)
            with pe.Fori(2, E - 1) as e:
                expert(e, False, False)
            expert(E - 1, False, True)
            down(E - 1, 0)
            down(E - 1, 1)


_INS = ["L0_attn_x", "L0_attn_wq", "L0_attn_wk", "L0_attn_wv", "L0_attn_wo", "L0_ffn_router_weight", "L0_ffn_router_bias",
        "L0_ffn_gate_up_proj", "L0_ffn_gate_up_proj_bias", "L0_ffn_down_proj", "L0_ffn_down_proj_bias"]


def _tables():
    half = D // 2
    freqs = np.power(np.float32(10000.0), -np.arange(half, dtype=np.float32) / np.float32(half)).astype(np.float32)
    rad = (freqs[:, None] * np.arange(T, dtype=np.float32)[None, :]).astype(np.float32)
    cos, sin = np.cos(rad).astype(np.float32), np.sin(rad).astype(np.float32)
    mask = np.zeros((P, T), np.float32)
    mask[:, P:] = np.where(np.arange(P)[None, :] > np.arange(P)[:, None], np.float32(NEG), np.float32(0.0))
    return {
        "rope_cos": np.concatenate([cos, cos], 0),
        "rope_sin": np.concatenate([-sin, sin], 0),
        "causal_mask": mask,
        "identity": np.eye(P, dtype=np.float32),
    }


def kernel(**inputs):
    import concourse.bacc as bacc
    from concourse.bass_utils import run_bass_kernel_spmd

    nc = bacc.Bacc("TRN2", target_bir_lowering=False, num_devices=1)
    arrays, args = {}, []
    given = {name: np.ascontiguousarray(inputs[name]) for name in _INS}
    for name, a in {**given, **_tables()}.items():
        arrays[f"in_{name}_dram"] = a
        args.append(nc.dram_tensor(f"in_{name}_dram", a.shape, mybir.dt.from_np(a.dtype), kind="ExternalInput").ap())
    args.append(nc.dram_tensor("out_0_dram", (B, T, M), F32, kind="ExternalOutput").ap())
    block_kernel(nc, *args)
    r = run_bass_kernel_spmd(nc, [arrays], core_ids=[0])
    return r.results[0]["out_0_dram"]
```

```python
from contextlib import ExitStack

import numpy as np

import concourse.bass as bass
from concourse import mybir

F32 = mybir.dt.float32
F32R = mybir.dt.float32r
ALU = mybir.AluOpType
ACT = mybir.ActivationFunctionType
AX_X = mybir.AxisListType.X

P = 128
B, T, M = 4, 256, 256
H, D = 16, 128
E, DF, TOP = 16, 256, 4
N = B * T
KM = M // P
TILES = N // P
HALF = N // 2
GROUPS = H // 2
PAIRS = 2 * B
QK_CHUNKS = 8
LEAD = 4
EPS = 1e-5
NEG = -1e30
ALPHA, LIMIT = 1.702, 7.0
NORM_COLS = 4 * B * 2
LAST = 4 * E - 1
SENTINEL = -3.0e38
FILL = 3.0e38


def pair_head(p):
    return (p // 2) % 2


def pair_batch(p):
    return 2 * (p // 4) + p % 2


def block_kernel(nc, x_d, wq_d, wk_d, wv_d, wo_d, rw_d, rb_d, gu_d, gub_d, dn_d, dnb_d,
                 rope_cos_d, rope_sin_d, mask_d, ident_d, out_d):
    ctx = ExitStack()
    with ctx:
        def sb(name, shape, dt=F32):
            return ctx.enter_context(nc.sbuf_tensor(name, shape, dt))

        def sem(name):
            return ctx.enter_context(nc.semaphore(name))

        x = sb("x", [P, TILES, M])
        xn = sb("xn", [P, TILES, M])
        xT_h = sb("xT_h", [P, KM, N], F32R)
        xT_l = sb("xT_l", [P, KM, N], F32R)
        attn = sb("attn", [P, TILES, M])
        moe = sb("moe", [P, TILES, M])
        rope_cos = sb("rope_cos", [P, T])
        rope_sin = sb("rope_sin", [P, T])
        mask = sb("mask", [P, T])
        ident = sb("ident", [P, P])
        stats = sb("stats", [P, TILES, 6])
        mean_var = sb("mean_var", [P, TILES, 2])
        var_eps = sb("var_eps", [P, NORM_COLS])
        minus_mean = sb("minus_mean", [P, NORM_COLS])
        rstd = sb("rstd", [P, NORM_COLS])
        shift = sb("shift", [P, NORM_COLS])
        minus_half = sb("minus_half", [P, 2])

        raw_qk = [sb(f"raw_qk{a}", [P, 2, KM, D]) for a in range(2)]
        qk_h = [sb(f"qk_h{a}", [P, 2, KM, D], F32R) for a in range(2)]
        qk_l = [sb(f"qk_l{a}", [P, 2, KM, D], F32R) for a in range(2)]
        raw_v = sb("raw_v", [P, KM, 2 * D])
        wv_h = sb("wv_h", [P, KM, 2 * D], F32R)
        wv_l = sb("wv_l", [P, KM, 2 * D], F32R)
        raw_o = [sb(f"raw_o{a}", [P, M]) for a in range(2)]
        wo_h = [sb(f"wo_h{a}", [P, M], F32R) for a in range(2)]
        wo_l = [sb(f"wo_l{a}", [P, M], F32R) for a in range(2)]
        qkT = sb("qkT", [P, 2, 4, HALF])
        V = sb("V", [P, B, 2, 2 * D])
        by_cos = sb("by_cos", [P, 2, HALF])
        by_sin = sb("by_sin", [P, 2, HALF])
        score = sb("score", [P, 2, P + T])
        row_bias = sb("row_bias", [P, 2, 2])
        row_sum = sb("row_sum", [P, 2, 2])
        row_rec = sb("row_rec", [P, 2, 2])
        prob = sb("prob", [P, 2, P + T])
        probT = sb("probT", [P, P + T])
        oT_h = sb("oT_h", [P, 2, T], F32R)
        oT_l = sb("oT_l", [P, 2, T], F32R)

        raw_gu = sb("raw_gu", [P, KM, 2 * DF])
        gu_h = [sb(f"gu_h{r}", [P, KM, 2, P], F32R) for r in range(2)]
        gu_l = [sb(f"gu_l{r}", [P, KM, 2, P], F32R) for r in range(2)]
        raw_dn = sb("raw_dn", [P, 2, M])
        dn_h = sb("dn_h", [P, 2, M], F32R)
        dn_l = sb("dn_l", [P, 2, M], F32R)
        gub_rows = sb("gub_rows", [2 * E, 2 * P])
        gate_bias = sb("gate_bias", [P, 2 * E])
        up_bias = sb("up_bias", [P, 2 * E])
        dnb = sb("dnb", [E, M])
        gate = sb("gate", [P, 2, HALF])
        glu = sb("glu", [P, 2, HALF])
        up = sb("up", [P, 2, HALF])
        act = sb("act", [P, 2, HALF])
        actT_h = sb("actT_h", [P, 2, N], F32R)
        actT_l = sb("actT_l", [P, 2, N], F32R)

        rw = sb("rw", [E, M])
        rwT_h = sb("rwT_h", [P, KM, E], F32R)
        rwT_l = sb("rwT_l", [P, KM, E], F32R)
        rb = sb("rb", [E, 1])
        logitsT = sb("logitsT", [E, N])
        logits = sb("logits", [P, TILES, E + 8])
        best = sb("best", [P, TILES, 8])
        marked = sb("marked", [P, TILES, E + 8])
        chosen = sb("chosen", [P, TILES, E])
        shifted = sb("shifted", [P, TILES, E])
        expo = sb("expo", [P, TILES, E])
        weight = sb("weight", [P, TILES, E])
        wsum = sb("wsum", [P, TILES])
        wrec = sb("wrec", [P, TILES])
        route = sb("route", [P, TILES, E])
        routeT = sb("routeT", [E, N])

        bank = [ctx.enter_context(nc.psum_tensor(f"bank{i}", [P, 512], F32)) for i in range(8)]
        ps_qk = bank[0:2]
        ps_s, ps_pT, ps_oT, ps_v = bank[2:6]
        ps_r = bank[6:8]
        ps_gu = [bank[0:2], bank[2:4]]
        ps_dn = [bank[4:6], bank[6:8]]

        XT_BANKS = [bank[i] for i in (2, 3, 4, 6, 5, 2, 4, 5)]

        dma_x = [sem(f"dma_x{u}") for u in range(4)]
        dma_ident = sem("dma_ident")
        dma_rope = sem("dma_rope")
        dma_mask = sem("dma_mask")
        dma_small = sem("dma_small")
        dma_qk = [sem(f"dma_qk{a}") for a in range(2)]
        dma_v = sem("dma_v")
        dma_o = [sem(f"dma_o{a}") for a in range(2)]
        dma_gu = sem("dma_gu")
        dma_dn = sem("dma_dn")
        dma_out = sem("dma_out")

        pool_const = sem("pool_const")
        pool_rstd = sem("pool_rstd")
        pool_shift = sem("pool_shift")
        pool_sin = sem("pool_sin")
        pool_qk = [sem(f"pool_qk{a}") for a in range(2)]
        pool_v = sem("pool_v")
        pool_o = [sem(f"pool_o{a}") for a in range(2)]
        pool_gu = [sem(f"pool_gu{r}") for r in range(2)]
        pool_dn = sem("pool_dn")
        pool_act = sem("pool_act")

        act_norm = sem("act_norm")
        act_x = sem("act_x")
        act_moe = sem("act_moe")
        act_xT = sem("act_xT")
        act_logits = sem("act_logits")
        act_swap = sem("act_swap")
        act_exp = sem("act_exp")
        act_pT = sem("act_pT")
        act_v = sem("act_v")
        act_oT = sem("act_oT")
        act_qk = [sem(f"act_qk{a}") for a in range(2)]
        act_wv = sem("act_wv")
        act_wo = [sem(f"act_wo{a}") for a in range(2)]
        act_gu = [sem(f"act_gu{r}") for r in range(2)]
        act_dn = sem("act_dn")
        act_glu = sem("act_glu")
        act_act = sem("act_act")
        act_small = sem("act_small")

        dve_stat = sem("dve_stat")
        dve_var = sem("dve_var")
        dve_xT = sem("dve_xT")
        dve_cos = sem("dve_cos")
        dve_rope = sem("dve_rope")
        dve_max = sem("dve_max")
        dve_rec = sem("dve_rec")
        dve_norm = sem("dve_norm")
        dve_oT = sem("dve_oT")
        dve_attn = sem("dve_attn")
        dve_small = sem("dve_small")
        dve_route = sem("dve_route")
        dve_routeT = sem("dve_routeT")
        dve_gate = sem("dve_gate")
        dve_up = sem("dve_up")
        dve_act = sem("dve_act")
        dve_moe = sem("dve_moe")
        dve_out = sem("dve_out")

        pe_xT = sem("pe_xT")
        pe_qk = sem("pe_qk")
        pe_s = sem("pe_s")
        pe_pT = sem("pe_pT")
        pe_oT = sem("pe_oT")
        pe_v = sem("pe_v")
        pe_r = sem("pe_r")
        pe_small = sem("pe_small")
        pe_logitsT = sem("pe_logitsT")
        pe_logits = sem("pe_logits")
        pe_routeT = sem("pe_routeT")
        pe_dnb = sem("pe_dnb")
        pe_gu = sem("pe_gu")
        pe_dn = sem("pe_dn")

        def halves_first(e):
            return isinstance(e, int) and e in (0, E - 1)

        def step_rc(e, q):
            return (q % 2, q // 2) if halves_first(e) else (q // 2, q % 2)

        NORMS = ([("x", u) for u in range(4)] + [("a", 0), ("a", 1), ("b", 0), ("b", 1), ("a", 2), ("a", 3), ("b", 2), ("b", 3)]
                 + [("moe", u) for u in range(4)])
        APPLIED = [n for n in NORMS if n[0] != "a"]
        V_CHUNK = {2: (0, 2), 3: (0, 3), 6: (1, 0), 7: (1, 1)}

        x_rows = x_d.rearrange("b (s p) m -> p (b s) m", p=P)
        out_rows = out_d.rearrange("b (s p) m -> p (b s) m", p=P)
        wq_cols = wq_d.rearrange("(k p) h d -> h p k d", p=P)
        wk_cols = wk_d.rearrange("(k p) h d -> h p k d", p=P)
        wv_cols = wv_d.rearrange("(k p) (g a) d -> g p k (a d)", p=P, a=2)
        gu_rows = gu_d.rearrange("e (k p) c -> e p k c", p=P)
        dn_rows = dn_d.rearrange("e (k p) m -> e p k m", p=P)

        block = ctx.enter_context(nc.Block())

        @block.sync
        def _(sp):
            def load_x(u):
                sp.dma_start(x[:, 2 * u:2 * u + 2, :], x_rows[:, 2 * u:2 * u + 2, :]).then_inc(dma_x[u], 16)

            def load_qk(a, g):
                sp.dma_start(raw_qk[a][:, 0, :, :], wq_cols[2 * g + a]).then_inc(dma_qk[a], 16)
                sp.dma_start(raw_qk[a][:, 1, :, :], wk_cols[2 * g + a]).then_inc(dma_qk[a], 16)

            def load_v(g):
                sp.dma_start(raw_v[:, :, :], wv_cols[g]).then_inc(dma_v, 16)

            def load_o(a, g):
                sp.dma_start(raw_o[a][:, :], wo_d[2 * g + a]).then_inc(dma_o[a], 16)

            load_x(0)
            load_x(1)
            load_qk(0, 0)
            sp.dma_start(ident[:, :], ident_d).then_inc(dma_ident, 16)
            load_x(2)
            sp.dma_start(rope_cos[:, :], rope_cos_d).then_inc(dma_rope, 16)
            sp.dma_start(rope_sin[:, :], rope_sin_d).then_inc(dma_rope, 16)
            load_qk(1, 0)
            load_x(3)
            load_v(0)
            sp.dma_start(mask[:, :], mask_d).then_inc(dma_mask, 16)
            load_o(0, 0)
            load_o(1, 0)
            sp.dma_start(rw[:, :], rw_d).then_inc(dma_small, 16)
            sp.dma_start(rb[:, :], rb_d.rearrange("(e o) -> e o", o=1)).then_inc(dma_small, 16)
            sp.dma_start(gub_rows[:, :], gub_d.rearrange("e (r c) -> (e r) c", r=2)).then_inc(dma_small, 16)
            sp.dma_start(dnb[:, :], dnb_d).then_inc(dma_small, 16)
            with sp.Fori(1, GROUPS) as g:
                sp.wait_ge(pool_qk[0], g)
                load_qk(0, g)
                sp.wait_ge(pool_qk[1], g)
                load_qk(1, g)
                sp.wait_ge(pool_v, g)
                load_v(g)
                sp.wait_ge(pool_o[0], g)
                load_o(0, g)
                sp.wait_ge(pool_o[1], g)
                load_o(1, g)
            sp.dma_start(raw_gu[:, :, :], gu_rows[0]).then_inc(dma_gu, 16)
            sp.dma_start(raw_dn[:, :, :], dn_rows[0]).then_inc(dma_dn, 16)
            with sp.Fori(1, E) as e:
                sp.wait_ge(pool_gu[0], e)
                sp.wait_ge(pool_gu[1], e)
                sp.dma_start(raw_gu[:, :, :], gu_rows[e]).then_inc(dma_gu, 16)
                sp.wait_ge(pool_dn, e)
                sp.dma_start(raw_dn[:, :, :], dn_rows[e]).then_inc(dma_dn, 16)
            for u in range(4):
                sp.wait_ge(dve_out, u + 1)
                sp.dma_start(out_rows[:, 2 * u:2 * u + 2, :], xn[:, 2 * u:2 * u + 2, :]).then_inc(dma_out, 16)
            sp.wait_ge(dma_out, 16 * 4)

        @block.gpsimd
        def _(pool):
            pool.memset(minus_half[:, :], -0.5).then_inc(pool_const, 1)
            pool.memset(attn[:, :, :], 0.0).then_inc(pool_const, 1)
            pool.memset(logits[:, :, E:E + 8], SENTINEL).then_inc(pool_const, 1)
            pool.wait_ge(pool_const, 1)

            def power(kind, u):
                n = NORMS.index((kind, u))
                cols = slice(2 * n, 2 * n + 2)
                pool.wait_ge(dve_var, n + 1)
                pool.tensor_tensor(rstd[:, cols], var_eps[:, cols], minus_half[:, :], ALU.pow).then_inc(pool_rstd, 1)
                pool.wait_ge(pool_rstd, n + 1)
                pool.tensor_tensor(shift[:, cols], minus_mean[:, cols], rstd[:, cols], ALU.mult).then_inc(pool_shift, 1)

            def low(out, raw, high, ready, n, done):
                pool.wait_ge(ready, n)
                pool.tensor_tensor(out, raw, high.bitcast(F32), ALU.subtract).then_inc(done, 1)

            def low_qk(a, g):
                low(qk_l[a][:, :, :, :], raw_qk[a][:, :, :, :], qk_h[a][:, :, :, :], act_qk[a], g + 1, pool_qk[a])

            def low_v(g):
                low(wv_l[:, :, :], raw_v[:, :, :], wv_h[:, :, :], act_wv, g + 1, pool_v)

            def low_o(a, g):
                low(wo_l[a][:, :], raw_o[a][:, :], wo_h[a][:, :], act_wo[a], g + 1, pool_o[a])

            def times_sine(n, w):
                pool.wait_ge(act_swap, n + 1)
                v = by_sin[:, w, :].rearrange("p (b t) -> p b t", b=2)
                pool.tensor_tensor(v, v, rope_sin[:, :].unsqueeze(1).broadcast_to([P, 2, T]), ALU.mult).then_inc(pool_sin, 1)

            def slot(g, p, last):
                if not (last and p >= QK_CHUNKS - LEAD):
                    times_sine(QK_CHUNKS * g + p + LEAD, p % 2)
                if p == 1:
                    low_o(1, g)
                if not last:
                    if p == 2:
                        low_qk(0, g + 1)
                    if p == 4:
                        low_qk(1, g + 1)
                    if p == 5:
                        low_v(g + 1)
                    if p == 7:
                        low_o(0, g + 1)

            power("x", 0)
            power("x", 1)
            low_qk(0, 0)
            power("x", 2)
            low_qk(1, 0)
            power("x", 3)
            low_v(0)
            pool.wait_ge(dma_rope, 32)
            for n in range(LEAD):
                times_sine(n, n % 2)
            low_o(0, 0)
            with pool.Fori(0, GROUPS - 1) as g:
                for p in range(PAIRS):
                    slot(g, p, False)
            for p in range(PAIRS):
                slot(GROUPS - 1, p, True)

            def gu_view(r):
                return raw_gu[:, :, :].rearrange("p k (d s) -> p k s d", s=2)[:, :, :, r * P:(r + 1) * P]

            def low_gu(r, e):
                low(gu_l[r][:, :, :, :], gu_view(r), gu_h[r][:, :, :, :], act_gu[r], e + 1, pool_gu[r])

            def low_dn(e):
                low(dn_l[:, :, :], raw_dn[:, :, :], dn_h[:, :, :], act_dn, e + 1, pool_dn)

            low_gu(0, 0)
            for kind, u in NORMS[4:12]:
                power(kind, u)
                if (kind, u) == ("a", 0):
                    low_gu(1, 0)
                if (kind, u) == ("a", 1):
                    low_dn(0)

            def low_act(e, q):
                r, c = step_rc(e, q)
                pool.wait_ge(act_act, 4 * e + q + 1)
                pool.tensor_tensor(actT_l[:, r, c * HALF:(c + 1) * HALF], act[:, q % 2, :],
                                   actT_h[:, r, c * HALF:(c + 1) * HALF].bitcast(F32),
                                   ALU.subtract).then_inc(pool_act, 1)

            def expert(e):
                low_gu(1, e)
                low_gu(0, e + 1)
                low_act(e, 0)
                low_act(e, 1)
                low_dn(e)
                low_act(e, 2)
                low_act(e, 3)

            for q in range(4):
                if q == 2:
                    low_gu(0, 1)
                low_act(0, q)
            with pool.Fori(1, E - 1) as e:
                expert(e)
            low_gu(1, E - 1)
            low_act(E - 1, 0)
            low_act(E - 1, 1)
            low_dn(E - 1)
            low_act(E - 1, 2)
            for b in range(2):
                cols = slice(HALF + b * T, HALF + (b + 1) * T)
                pool.wait_ge(act_act, LAST + b + 1)
                pool.tensor_tensor(actT_l[:, 1, cols], act[:, 1, b * T:(b + 1) * T], actT_h[:, 1, cols].bitcast(F32),
                                   ALU.subtract).then_inc(pool_act, 1)
            for u in range(4):
                power("moe", u)

        @block.scalar
        def _(sc):
            def copy(out, in_):
                return sc.activation(out, in_, ACT.Copy)

            def high_qk(a, g, free=True):
                sc.wait_ge(dma_qk[a], 32 * g + 32)
                if free:
                    sc.wait_ge(pe_qk, QK_CHUNKS * g - 2 + 2 * a)
                copy(qk_h[a][:, :, :, :], raw_qk[a][:, :, :, :]).then_inc(act_qk[a], 1)

            def high_v(g, free=True):
                sc.wait_ge(dma_v, 16 * g + 16)
                if free:
                    sc.wait_ge(pe_v, 4 * g)
                copy(wv_h[:, :, :], raw_v[:, :, :]).then_inc(act_wv, 1)

            def high_o(a, g, free=True):
                sc.wait_ge(dma_o[a], 16 * g + 16)
                if free:
                    sc.wait_ge(pe_r, PAIRS * g - (0 if a else 2))
                copy(wo_h[a][:, :], raw_o[a][:, :]).then_inc(act_wo[a], 1)

            def swap(n, w):
                sc.wait_ge(dve_cos, n + 1)
                if not (isinstance(n, int) and n < 2):
                    sc.wait_ge(dve_rope, n - 1)
                copy(by_sin[0:64, w, :], ps_qk[w][64:128, :])
                copy(by_sin[64:128, w, :], ps_qk[w][0:64, :]).then_inc(act_swap, 1)

            def softmax_exp(g, p):
                k = PAIRS * g + p
                sc.wait_ge(dve_max, k + 1)
                if not (isinstance(k, int) and k < 2):
                    sc.wait_ge(pe_pT, k - 1)
                for i, (lo, hi) in enumerate([(0, P), (P, P + T)]):
                    e = sc.activation(prob[:, p % 2, lo:hi], score[:, p % 2, lo:hi], ACT.Exp,
                                      bias=row_bias[:, p % 2, i:i + 1], scale=-1.0,
                                      accum_out=row_sum[:, p % 2, i:i + 1])
                e.then_inc(act_exp, 1)

            def values(m, b, free):
                sc.wait_ge(pe_v, m + 1)
                if free is not None:
                    sc.wait_ge(pe_oT, free)
                copy(V[:, b, :, :], ps_v[:, :].rearrange("p (s c) -> p s c", s=2)).then_inc(act_v, 1)

            def oT_high(g, p):
                k = PAIRS * g + p
                sc.wait_ge(pe_oT, k + 1)
                if not (isinstance(k, int) and k < 2):
                    sc.wait_ge(pe_r, k - 1)
                copy(oT_h[:, p % 2, :], ps_oT[:, 0:T]).then_inc(act_oT, 1)

            def probT_out(g, p):
                sc.wait_ge(pe_pT, PAIRS * g + p + 1)
                copy(probT[:, :], ps_pT[:, 0:P + T]).then_inc(act_pT, 1)

            def slot(g, p, first, last):
                if not (first and p == 0):
                    oT_high(g - (p == 0), (p - 1) % PAIRS)
                if not (last and p == PAIRS - 1):
                    softmax_exp(g + (p == PAIRS - 1), (p + 1) % PAIRS)
                probT_out(g, p)
                if not (last and p >= QK_CHUNKS - LEAD):
                    swap(QK_CHUNKS * g + p + LEAD, p % 2)
                if p in V_CHUNK and not (last and V_CHUNK[p][0]):
                    dg, b = V_CHUNK[p]
                    free = None if first and not dg else PAIRS * (g + dg - 1) + 4 * (b // 2) + 2 + b % 2 + 1
                    values(4 * (g + dg) + b, b, free)
                if p == 1:
                    high_o(1, g, not first)
                if not last:
                    if p == 2:
                        high_qk(0, g + 1)
                    if p == 4:
                        high_qk(1, g + 1)
                    if p == 5:
                        high_v(g + 1)
                    if p == 7:
                        high_o(0, g + 1)

            def normalise(kind, u, out, src, each_tile=None):
                n = NORMS.index((kind, u))
                sc.wait_ge(pool_shift, n + 1)
                for i in range(2):
                    m = sc.activation(out[:, 2 * u + i, :], src[:, 2 * u + i, :], ACT.Identity,
                                      bias=shift[:, 2 * n + i:2 * n + i + 1], scale=rstd[:, 2 * n + i:2 * n + i + 1])
                    if each_tile is not None:
                        m.then_inc(each_tile, 1)
                if each_tile is None:
                    m.then_inc(act_norm, 1)

            def shift_x(u):
                n = NORMS.index(("a", u))
                sc.wait_ge(pool_shift, n + 1)
                for i in range(2):
                    m = sc.activation(x[:, 2 * u + i, :], x[:, 2 * u + i, :], ACT.Identity, bias=shift[:, 2 * n + i:2 * n + i + 1])
                m.then_inc(act_x, 1)

            def xT_high(n, bank_of):
                sc.wait_ge(pe_xT, n + 1)
                c = (n % 4) * T
                copy(xT_h[:, :, c:c + T], bank_of[:, :].rearrange("p (k t) -> p k t", k=KM)).then_inc(act_xT, 1)

            normalise("x", 0, xn, x)
            high_qk(0, 0, False)
            normalise("x", 1, xn, x)
            xT_high(0, XT_BANKS[0])
            xT_high(1, XT_BANKS[1])
            high_qk(1, 0, False)
            normalise("x", 2, xn, x)
            high_v(0, False)
            normalise("x", 3, xn, x)
            swap(0, 0)
            xT_high(2, XT_BANKS[2])
            swap(1, 1)
            values(0, 0, None)
            xT_high(3, XT_BANKS[3])
            swap(2, 0)
            swap(3, 1)
            values(1, 1, None)
            high_o(0, 0, False)
            softmax_exp(0, 0)
            for p in range(PAIRS):
                slot(0, p, True, False)
            with sc.Fori(1, GROUPS - 1) as g:
                for p in range(PAIRS):
                    slot(g, p, False, False)
            def gu_view(r):
                return raw_gu[:, :, :].rearrange("p k (d s) -> p k s d", s=2)[:, :, :, r * P:(r + 1) * P]

            def high_gu(r, e, free=True):
                sc.wait_ge(dma_gu, 16 * e + 16)
                if free:
                    sc.wait_ge(pe_gu, 3 if isinstance(e, int) and e == 1 and r == 0 else 4 * e - 2 + 2 * r)
                for k in range(KM):
                    c = copy(gu_h[r][:, k, :, :], gu_view(r)[:, k, :, :])
                c.then_inc(act_gu[r], 1)

            def high_dn(e, free=True):
                sc.wait_ge(dma_dn, 16 * e + 16)
                if free:
                    sc.wait_ge(pe_dn, 4 * e)
                copy(dn_h[:, :, :], raw_dn[:, :, :]).then_inc(act_dn, 1)

            for p in range(4):
                slot(GROUPS - 1, p, False, True)
            for p in range(4, PAIRS):
                oT_high(GROUPS - 1, p - 1)
                if p == 4:
                    softmax_exp(GROUPS - 1, p + 1)
                probT_out(GROUPS - 1, p)
                if p + 2 < PAIRS:
                    softmax_exp(GROUPS - 1, p + 2)
                if p in (4, 6):
                    high_gu((p - 4) // 2, 0, False)
                if p == 7:
                    high_dn(0, False)
            oT_high(GROUPS - 1, PAIRS - 1)

            def gelu(e, q, first):
                s = 4 * e + q
                sc.wait_ge(dve_gate, s + 1)
                if not (first and q < 2):
                    sc.wait_ge(dve_act, s - 1)
                sc.activation(glu[:, q % 2, :], gate[:, q % 2, :], ACT.Gelu_apprx_sigmoid).then_inc(act_glu, 1)

            def act_high(e, q, first):
                s = 4 * e + q
                r, c = step_rc(e, q)
                sc.wait_ge(dve_act, s + 1)
                if not first:
                    sc.wait_ge(pe_dn, 4 * (e - 1) + 2 * c + 2)
                copy(actT_h[:, r, c * HALF:(c + 1) * HALF], act[:, q % 2, :]).then_inc(act_act, 1)

            def expert(e):
                high_gu(1, e)
                gelu(e, 0, False)
                gelu(e, 1, False)
                high_gu(0, e + 1)
                act_high(e, 0, False)
                gelu(e, 2, False)
                act_high(e, 1, False)
                high_dn(e)
                act_high(e, 2, False)
                gelu(e, 3, False)
                act_high(e, 3, False)

            normalise("b", 0, xn, x)
            xT_high(4, XT_BANKS[4])
            normalise("b", 1, xn, x)
            xT_high(5, XT_BANKS[5])
            normalise("b", 2, xn, x)
            normalise("b", 3, xn, x)
            xT_high(6, XT_BANKS[6])
            xT_high(7, XT_BANKS[7])
            gelu(0, 0, True)
            act_high(0, 0, True)
            gelu(0, 1, True)
            act_high(0, 1, True)
            for c in range(2):
                sc.wait_ge(pe_logitsT, c + 1)
                sc.activation(logitsT[:, c * HALF:(c + 1) * HALF], bank[6 + c][0:E, :], ACT.Identity,
                              bias=rb[:, 0:1]).then_inc(act_logits, 1)
            high_gu(0, 1)
            gelu(0, 2, True)
            sc.wait_ge(dve_small, 8)
            sc.activation(expo[:, :, :], shifted[:, :, :], ACT.Exp).then_inc(act_small, 1)
            act_high(0, 2, True)
            gelu(0, 3, True)
            act_high(0, 3, True)
            with sc.Fori(1, E - 1) as e:
                expert(e)
            high_gu(1, E - 1)
            for q in range(3):
                gelu(E - 1, q, False)
                act_high(E - 1, q, False)
                if q == 1:
                    high_dn(E - 1)
                shift_x(q)
            sc.wait_ge(dve_act, LAST - 1)
            for b in range(2):
                cols = slice(b * T, (b + 1) * T)
                sc.wait_ge(dve_gate, LAST + b + 1)
                sc.activation(glu[:, 1, cols], gate[:, 1, cols], ACT.Gelu_apprx_sigmoid).then_inc(act_glu, 1)
            for b in range(2):
                sc.wait_ge(dve_act, LAST + b + 1)
                copy(actT_h[:, 1, HALF + b * T:HALF + (b + 1) * T], act[:, 1, b * T:(b + 1) * T]).then_inc(act_act, 1)
            shift_x(3)
            for u in range(4):
                normalise("moe", u, moe, moe, act_moe)

        @block.vector
        def _(dve):
            steps = [0]

            def chain(ins):
                steps[0] += 1
                ins.then_inc(dve_stat, 1)
                dve.wait_ge(dve_stat, steps[0])

            def row_stats(src, kind, u):
                n = NORMS.index((kind, u))
                tiles = slice(2 * u, 2 * u + 2)
                for t in (2 * u, 2 * u + 1):
                    steps[0] += 1
                    dve.bn_stats(stats[:, t, :], src[:, t, :]).then_inc(dve_stat, 1)
                for t in (2 * u, 2 * u + 1):
                    dve.wait_ge(dve_stat, steps[0] - 1 + t % 2)
                    s = dve.bn_aggr(mean_var[:, t, :], stats[:, t, :])
                chain(s)
                cols = slice(2 * n, 2 * n + 2)
                dve.tensor_scalar(minus_mean[:, cols], mean_var[:, tiles, 0], -1.0, None, ALU.mult)
                dve.tensor_scalar(var_eps[:, cols], mean_var[:, tiles, 1], EPS, None, ALU.add).then_inc(dve_var, 1)

            def xT_low(n):
                dve.wait_ge(act_xT, n + 1)
                c = (n % 4) * T
                dve.tensor_tensor(xT_l[:, :, c:c + T], XT_BANKS[n][:, :].rearrange("p (k t) -> p k t", k=KM),
                                  xT_h[:, :, c:c + T].bitcast(F32), ALU.subtract).then_inc(dve_xT, 1)

            for u in range(4):
                dve.wait_ge(dma_x[u], 16)
                row_stats(x, "x", u)
                if u == 2:
                    xT_low(0)
                    xT_low(1)

            def cosine(n, w):
                dve.wait_ge(pe_qk, n + 1)
                if not (isinstance(n, int) and n < 2):
                    dve.wait_ge(dve_rope, n - 1)
                v = by_cos[:, w, :].rearrange("p (b t) -> p b t", b=2)
                dve.tensor_tensor(v, ps_qk[w][:, :].rearrange("p (b t) -> p b t", b=2),
                                  rope_cos[:, :].unsqueeze(1).broadcast_to([P, 2, T]), ALU.mult).then_inc(dve_cos, 1)

            def rotate(n, w, j, free):
                dve.wait_ge(pool_sin, n + 1)
                dve.wait_ge(dve_cos, n + 1)
                if free is not None:
                    dve.wait_ge(pe_s, free)
                dve.tensor_tensor(qkT[:, w, j, :], by_cos[:, w, :], by_sin[:, w, :], ALU.add).then_inc(dve_rope, 1)

            def await_scores(g, p):
                k = PAIRS * g + p
                dve.wait_ge(pe_s, k + 1)
                if not (isinstance(k, int) and k < 2):
                    dve.wait_ge(act_exp, k - 1)
                dve.memset(row_sum[:, p % 2, :], 0.0)

            def row_max(p):
                for i, (lo, hi) in enumerate([(0, P), (P, P + T)]):
                    m = dve.tensor_tensor_reduce(score[:, p % 2, lo:hi], ps_s[:, lo:hi], mask[:, P:T] if i == 0 else mask[:, :],
                                                 -1.0 / D, FILL, ALU.add, ALU.min, row_bias[:, p % 2, i:i + 1])
                m.then_inc(dve_max, 1)

            def normalise_prob(g, p):
                k = PAIRS * g + p
                dve.wait_ge(act_exp, k + 1)
                dve.reciprocal(row_rec[:, p % 2, :], row_sum[:, p % 2, :]).then_inc(dve_rec, 1)
                dve.wait_ge(dve_rec, k + 1)
                for i, (lo, hi) in enumerate([(0, P), (P, P + T)]):
                    m = dve.tensor_scalar(prob[:, p % 2, lo:hi], prob[:, p % 2, lo:hi], row_rec[:, p % 2, i:i + 1],
                                          None, ALU.mult)
                m.then_inc(dve_norm, 1)

            def oT_low(g, p):
                dve.wait_ge(act_oT, PAIRS * g + p + 1)
                dve.tensor_tensor(oT_l[:, p % 2, :], ps_oT[:, 0:T], oT_h[:, p % 2, :].bitcast(F32),
                                  ALU.subtract).then_inc(dve_oT, 1)

            def add_attn(g, p):
                dve.wait_ge(pe_r, PAIRS * g + p + 1)
                b = pair_batch(p)
                v = attn[:, 2 * b:2 * b + 2, :]
                dve.tensor_tensor(v, ps_r[b % 2][:, :].rearrange("p (s m) -> p s m", s=2), v, ALU.add).then_inc(dve_attn, 1)

            def slot(g, p, first, last):
                if not (last and p == PAIRS - 1):
                    await_scores(g + (p == PAIRS - 1), (p + 1) % PAIRS)
                    row_max((p + 1) % PAIRS)
                if not (first and p == 0):
                    oT_low(g - (p == 0), (p - 1) % PAIRS)
                if not (last and p > QK_CHUNKS - LEAD):
                    n, unit = QK_CHUNKS * g + p + LEAD - 1, (p + LEAD - 1) // 2
                    free = None if first and unit < 4 else PAIRS * g + 2 * unit - 6
                    rotate(n, (p + 1) % 2, unit % 4, free)
                if not (last and p >= QK_CHUNKS - LEAD):
                    cosine(QK_CHUNKS * g + p + LEAD, p % 2)
                if not (last and p == PAIRS - 1):
                    normalise_prob(g + (p == PAIRS - 1), (p + 1) % PAIRS)
                if not (first and p < 2) and pair_head((p - 2) % PAIRS):
                    add_attn(g - (p < 2), (p - 2) % PAIRS)

            dve.wait_ge(dma_rope, 32)
            for n in range(LEAD):
                cosine(n, n % 2)
                if n in (1, 2):
                    rotate(n - 1, n - 1, 0, None)
                    xT_low(n + 1)
            await_scores(0, 0)
            dve.wait_ge(dma_mask, 16)
            row_max(0)
            rotate(2, 0, 1, None)
            normalise_prob(0, 0)
            dve.wait_ge(pool_const, 3)
            for p in range(PAIRS):
                slot(0, p, True, False)
            with dve.Fori(1, GROUPS - 1) as g:
                for p in range(PAIRS):
                    slot(g, p, False, False)

            def attn_stats(u):
                dve.wait_ge(dve_attn, 4 * (GROUPS - 1) + u + 1)
                row_stats(attn, "a", u)

            def residual(u):
                n = NORMS.index(("a", u))
                dve.wait_ge(pool_rstd, n + 1)
                for i in range(2):
                    m = dve.scalar_tensor_tensor(out=x[:, 2 * u + i, :], in0=attn[:, 2 * u + i, :],
                                                 scalar=rstd[:, 2 * n + i:2 * n + i + 1], in1=x[:, 2 * u + i, :],
                                                 op0=ALU.mult, op1=ALU.add)
                chain(m)
                row_stats(x, "b", u)

            def small_tables():
                dve.wait_ge(pe_small, 1)
                dve.tensor_copy(gate_bias[:, :], ps_v[:, 0:2 * E])
                dve.tensor_scalar(up_bias[:, :], ps_v[:, 2 * E:4 * E], 1.0, None, ALU.add)
                dve.tensor_copy(rwT_h[:, :, :], ps_v[:, 4 * E:6 * E].rearrange("p (k e) -> p k e", k=KM)).then_inc(dve_small, 1)
                dve.wait_ge(dve_small, 1)
                dve.tensor_tensor(rwT_l[:, :, :], ps_v[:, 4 * E:6 * E].rearrange("p (k e) -> p k e", k=KM),
                                  rwT_h[:, :, :].bitcast(F32), ALU.subtract).then_inc(dve_small, 1)

            for p in range(4):
                slot(GROUPS - 1, p, False, True)
            for p in range(4, PAIRS):
                ahead = p + (1 if p == 4 else 2)
                if ahead < PAIRS:
                    await_scores(GROUPS - 1, ahead)
                    row_max(ahead)
                if p == 5:
                    small_tables()
                oT_low(GROUPS - 1, p - 1)
                if p == 4:
                    rotate(QK_CHUNKS * GROUPS - 1, 1, 3, PAIRS * GROUPS - 8)
                if p + 1 < PAIRS:
                    normalise_prob(GROUPS - 1, p + 1)
                if p == 4:
                    await_scores(GROUPS - 1, p + 2)
                    row_max(p + 2)
                if p < 6:
                    add_attn(GROUPS - 1, p - 2)
                if p in (5, 6):
                    attn_stats(p - 5)
            residual(0)
            oT_low(GROUPS - 1, PAIRS - 1)
            residual(1)
            add_attn(GROUPS - 1, PAIRS - 2)
            attn_stats(2)
            xT_low(4)
            add_attn(GROUPS - 1, PAIRS - 1)
            attn_stats(3)
            xT_low(5)
            residual(2)
            residual(3)

            def router():
                dve.wait_ge(pe_logits, 1)
                dve.tensor_copy(logits[:, :, 0:E], bank[6][:, 0:TILES * E].rearrange("p (t e) -> p t e", e=E)).then_inc(dve_small, 1)
                dve.wait_ge(dve_small, 3)
                for t in range(TILES):
                    m = dve.max(best[:, t, :], logits[:, t, 0:E])
                m.then_inc(dve_small, 1)
                dve.wait_ge(dve_small, 4)
                dve.memset(best[:, :, TOP:8], SENTINEL).then_inc(dve_small, 1)
                dve.wait_ge(dve_small, 5)
                for t in range(TILES):
                    m = dve.match_replace(marked[:, t, :], best[:, t, :], logits[:, t, :], FILL)
                m.then_inc(dve_small, 1)
                dve.wait_ge(dve_small, 6)
                dve.tensor_tensor(chosen[:, :, :], marked[:, :, 0:E], logits[:, :, 0:E], ALU.not_equal).then_inc(dve_small, 1)
                dve.tensor_tensor(shifted[:, :, :], logits[:, :, 0:E], best[:, :, 0:1].broadcast_to([P, TILES, E]),
                                  ALU.subtract).then_inc(dve_small, 1)
                dve.wait_ge(act_small, 1)
                dve.wait_ge(dve_small, 8)
                dve.tensor_tensor(weight[:, :, :], expo[:, :, :], chosen[:, :, :], ALU.mult).then_inc(dve_small, 1)
                dve.wait_ge(dve_small, 9)
                dve.tensor_reduce(wsum[:, :], weight[:, :, :], AX_X, ALU.add).then_inc(dve_small, 1)
                dve.wait_ge(dve_small, 10)
                dve.reciprocal(wrec[:, :], wsum[:, :]).then_inc(dve_small, 1)
                dve.wait_ge(dve_small, 11)
                dve.tensor_tensor(route[:, :, :], weight[:, :, :], wrec[:, :].unsqueeze(2).broadcast_to([P, TILES, E]),
                                  ALU.mult).then_inc(dve_route, 1)

            def turned_route():
                for c in range(2):
                    dve.wait_ge(pe_routeT, c + 1)
                    dve.tensor_copy(routeT[:, c * HALF:(c + 1) * HALF], bank[4 + c][0:E, :]).then_inc(dve_routeT, 1)

            def start_moe():
                for u in range(4):
                    dve.wait_ge(pe_dnb, u + 1)
                    dve.tensor_copy(moe[:, 2 * u:2 * u + 2, :], bank[4 + u][:, :].rearrange("p (s m) -> p s m", s=2)).then_inc(dve_moe, 1)
                dve.wait_ge(dve_moe, 4)

            def add_moe(e, c, batches=(0, 1)):
                for w in batches:
                    dve.wait_ge(pe_dn, 4 * e + 2 * c + w + 1)
                    if not (isinstance(e, int) and e == 0):
                        dve.wait_ge(dve_moe, 4 * e + 2 * c + w + 1)
                    for s in range(2):
                        t = 4 * c + 2 * w + s
                        m = dve.scalar_tensor_tensor(out=moe[:, t, :], in0=ps_dn[c][w][:, s * M:(s + 1) * M],
                                                     scalar=route[:, t, bass.ds(e, 1)], in1=moe[:, t, :],
                                                     op0=ALU.mult, op1=ALU.add)
                    m.then_inc(dve_moe, 1)

            def clamp(e, q, first):
                s = 4 * e + q
                r, _ = step_rc(e, q)
                dve.wait_ge(pe_gu, s + 1)
                if not (first and q < 2):
                    dve.wait_ge(act_glu, s - 1)
                dve.tensor_scalar(gate[:, q % 2, :], ps_gu[q % 2][0][:, :], gate_bias[:, bass.ds(2 * e + r, 1)], LIMIT,
                                  ALU.add, ALU.min).then_inc(dve_gate, 1)
                if not (first and q < 2):
                    dve.wait_ge(dve_act, s - 1)
                dve.tensor_scalar(up[:, q % 2, :], ps_gu[q % 2][1][:, :], up_bias[:, bass.ds(2 * e + r, 1)], 1.0 - LIMIT,
                                  ALU.add, ALU.max).then_inc(dve_up, 1)

            def gated(e, q, first):
                s = 4 * e + q
                dve.wait_ge(act_glu, s + 1)
                dve.wait_ge(dve_up, s + 1)
                if not (first and q < 2):
                    dve.wait_ge(pool_act, s - 1)
                dve.scalar_tensor_tensor(out=act[:, q % 2, :], in0=up[:, q % 2, :], scalar=1.0 + LIMIT,
                                         in1=glu[:, q % 2, :], op0=ALU.min, op1=ALU.mult).then_inc(dve_act, 1)

            def expert(e):
                for q in range(4):
                    clamp(e, q, False)
                    gated(e, q, False)
                    if q in (1, 2):
                        add_moe(e - 1, q - 1)

            clamp(0, 0, True)
            xT_low(6)
            xT_low(7)
            gated(0, 0, True)
            clamp(0, 1, True)
            gated(0, 1, True)
            clamp(0, 2, True)
            gated(0, 2, True)
            router()
            clamp(0, 3, True)
            gated(0, 3, True)
            turned_route()
            clamp(1, 0, False)
            gated(1, 0, False)
            clamp(1, 1, False)
            gated(1, 1, False)
            start_moe()
            add_moe(0, 0)
            clamp(1, 2, False)
            gated(1, 2, False)
            add_moe(0, 1)
            clamp(1, 3, False)
            gated(1, 3, False)
            with dve.Fori(2, E - 1) as e:
                expert(e)

            for q in range(3):
                clamp(E - 1, q, False)
                gated(E - 1, q, False)
                if q < 2:
                    add_moe(E - 2, q)

            def last_gate(b):
                cols = slice(b * T, (b + 1) * T)
                dve.tensor_scalar(gate[:, 1, cols], ps_gu[1][0][:, cols], gate_bias[:, 2 * E - 1:2 * E], LIMIT,
                                  ALU.add, ALU.min).then_inc(dve_gate, 1)

            def last_up(b):
                cols = slice(b * T, (b + 1) * T)
                dve.tensor_scalar(up[:, 1, cols], ps_gu[1][1][:, cols], up_bias[:, 2 * E - 1:2 * E], 1.0 - LIMIT,
                                  ALU.add, ALU.max).then_inc(dve_up, 1)

            def last_gated(b):
                cols = slice(b * T, (b + 1) * T)
                dve.wait_ge(act_glu, LAST + b + 1)
                dve.wait_ge(dve_up, LAST + b + 1)
                dve.scalar_tensor_tensor(out=act[:, 1, cols], in0=up[:, 1, cols], scalar=1.0 + LIMIT,
                                         in1=glu[:, 1, cols], op0=ALU.min, op1=ALU.mult).then_inc(dve_act, 1)

            dve.wait_ge(pe_gu, LAST + 1)
            dve.wait_ge(act_glu, LAST - 1)
            last_gate(0)
            dve.wait_ge(dve_act, LAST - 1)
            last_up(0)
            last_gate(1)
            dve.wait_ge(pool_act, LAST - 1)
            last_gated(0)
            last_up(1)
            last_gated(1)

            def finish(u):
                dve.wait_ge(act_x, u + 1)
                for t in (2 * u, 2 * u + 1):
                    dve.wait_ge(act_moe, t + 1)
                    m = dve.tensor_tensor(xn[:, t, :], moe[:, t, :], x[:, t, :], ALU.add)
                m.then_inc(dve_out, 1)

            for u in range(4):
                add_moe(E - 1, u // 2, [u % 2])
                dve.wait_ge(dve_moe, 4 * E + u + 1)
                row_stats(moe, "moe", u)
                if u == 1:
                    finish(0)
            for u in range(1, 4):
                finish(u)

        @block.tensor
        def _(pe):
            def product(out, pairs, first=True, last=True):
                terms = [t for lh, ll, rh, rl in pairs for t in ((lh, rh), (lh, rl), (ll, rh))]
                for i, (lhs, rhs) in enumerate(terms):
                    m = pe.matmul(out, lhs, rhs, start=first and i == 0, stop=last and i == len(terms) - 1,
                                  skip_group_check=not (first and last))
                return m

            def turn_rows(kind, u, n):
                pe.wait_ge(act_norm, APPLIED.index((kind, u)) + 1)
                for s in range(2):
                    for k in range(KM):
                        m = pe.transpose(XT_BANKS[n][:, k * T + s * P:k * T + (s + 1) * P],
                                         xn[:, 2 * u + s, k * P:(k + 1) * P], ident[:, :])
                m.then_inc(pe_xT, 1)

            def qk_chunk(n, w, a, c, group, free):
                pe.wait_ge(pool_qk[a], group + 1)
                if free:
                    pe.wait_ge(act_swap, n - 1)
                cols = slice(c * HALF, (c + 1) * HALF)
                product(ps_qk[w][:, :], [(qk_h[a][:, w, k, :], qk_l[a][:, w, k, :], xT_h[:, k, cols], xT_l[:, k, cols])
                                         for k in range(KM)]).then_inc(pe_qk, 1)

            def v_chunk(m, b, group, free):
                pe.wait_ge(pool_v, group + 1)
                if free:
                    pe.wait_ge(act_v, m)
                for s in range(2):
                    cols = slice((2 * b + s) * P, (2 * b + s + 1) * P)
                    v = product(ps_v[:, s * T:(s + 1) * T], [(xT_h[:, k, cols], xT_l[:, k, cols], wv_h[:, k, :], wv_l[:, k, :])
                                                             for k in range(KM)])
                v.then_inc(pe_v, 1)

            def scores(g, p, free):
                j, o = p // 2, (p % 2) * T
                if p % 2 == 0:
                    pe.wait_ge(dve_rope, QK_CHUNKS * g + 2 * j + 2)
                if free:
                    pe.wait_ge(dve_max, PAIRS * g + p)
                pe.matmul(ps_s[:, 0:P], qkT[:, 0, j, o:o + P], qkT[:, 1, j, o:o + P], start=True, stop=True)
                pe.matmul(ps_s[:, P:P + T], qkT[:, 0, j, o + P:o + T], qkT[:, 1, j, o:o + T],
                          start=True, stop=True).then_inc(pe_s, 1)

            def turn_prob(g, p, free):
                pe.wait_ge(dve_norm, PAIRS * g + p + 1)
                if free:
                    pe.wait_ge(act_pT, PAIRS * g + p)
                for i in range(3):
                    m = pe.transpose(ps_pT[:, i * P:(i + 1) * P], prob[:, p % 2, i * P:(i + 1) * P], ident[:, :])
                m.then_inc(pe_pT, 1)

            def weigh_values(g, p, free):
                a, b = pair_head(p), pair_batch(p)
                pe.wait_ge(act_pT, PAIRS * g + p + 1)
                pe.wait_ge(act_v, 4 * g + b + 1)
                if free:
                    pe.wait_ge(dve_oT, PAIRS * g + p)
                pe.matmul(ps_oT[:, 0:T], V[:, b, 0, a * D:(a + 1) * D], probT[:, 0:T], start=True, stop=False,
                          skip_group_check=True)
                pe.matmul(ps_oT[:, P:T], V[:, b, 1, a * D:(a + 1) * D], probT[:, T:T + P], start=False, stop=True,
                          skip_group_check=True).then_inc(pe_oT, 1)

            def output_rows(g, p, first):
                a, b = pair_head(p), pair_batch(p)
                pe.wait_ge(dve_oT, PAIRS * g + p + 1)
                pe.wait_ge(pool_o[a], g + 1)
                if a == 0 and not (first and p < 2):
                    pe.wait_ge(dve_attn, 4 * g + 2 * (p // 4) + p % 2 - 1)
                for s in range(2):
                    m = product(ps_r[b % 2][:, s * M:(s + 1) * M],
                                [(oT_h[:, p % 2, s * P:(s + 1) * P], oT_l[:, p % 2, s * P:(s + 1) * P], wo_h[a][:, :], wo_l[a][:, :])],
                                first=(a == 0 and s == 0), last=(a == 1))
                m.then_inc(pe_r, 1)

            def slot(g, p, first, last):
                if not (last and p >= QK_CHUNKS - LEAD):
                    unit = (p + LEAD) // 2
                    qk_chunk(QK_CHUNKS * g + p + LEAD, p % 2, unit % 2, (unit // 2) % 2, g + (unit >= 4), True)
                early = last and p > QK_CHUNKS - LEAD
                if early and p < PAIRS - 2:
                    scores(g, p + 2, True)
                turn_prob(g, p, not (first and p == 0))
                if not (first and p == 0):
                    output_rows(g - (p == 0), (p - 1) % PAIRS, first and p != 0)
                if not early:
                    scores(g + (p >= PAIRS - 2), (p + 2) % PAIRS, True)
                if p in V_CHUNK and not (last and V_CHUNK[p][0]):
                    dg, b = V_CHUNK[p]
                    v_chunk(4 * (g + dg) + b, b, g + dg, True)
                weigh_values(g, p, not (first and p == 0))

            pe.wait_ge(dma_ident, 16)
            turn_rows("x", 0, 0)
            turn_rows("x", 1, 1)
            pe.wait_ge(pool_qk[0], 1)
            for b in range(2):
                pe.wait_ge(dve_xT, b + 1)
                cols = slice(b * T, (b + 1) * T)
                for w in range(2):
                    m = product(ps_qk[w][:, cols], [(qk_h[0][:, w, k, :], qk_l[0][:, w, k, :], xT_h[:, k, cols], xT_l[:, k, cols])
                                                    for k in range(KM)])
                    if b == 1:
                        m.then_inc(pe_qk, 1)
            turn_rows("x", 2, 2)
            v_chunk(0, 0, 0, False)
            qk_chunk(2, 0, 1, 0, 0, True)
            turn_rows("x", 3, 3)
            qk_chunk(3, 1, 1, 0, 0, True)
            v_chunk(1, 1, 0, True)
            pe.wait_ge(dve_xT, 4)
            scores(0, 0, False)
            pe.wait_ge(dve_xT, 4)
            scores(0, 1, True)
            for p in range(PAIRS):
                slot(0, p, True, False)
            with pe.Fori(1, GROUPS - 1) as g:
                for p in range(PAIRS):
                    slot(g, p, False, False)
            for p in range(PAIRS):
                slot(GROUPS - 1, p, False, True)
                if p == 4:
                    pe.wait_ge(act_v, 4 * GROUPS)
                    pe.wait_ge(dma_small, 64)
                    for s in range(2):
                        rows = gub_rows[:, :].rearrange("q (d s) -> q s d", s=2)[:, s, :]
                        pe.transpose(ps_v[:, s * 2 * E:(s + 1) * 2 * E], rows, ident[0:2 * E, 0:2 * E])
                    for k in range(KM):
                        m = pe.transpose(ps_v[:, (4 + k) * E:(5 + k) * E], rw[:, k * P:(k + 1) * P], ident[0:E, 0:E])
                    m.then_inc(pe_small, 1)
            output_rows(GROUPS - 1, PAIRS - 1, False)

            def gate_up(e, q, free):
                r, c = step_rc(e, q)
                pe.wait_ge(pool_gu[r], e + 1)
                if free:
                    pe.wait_ge(dve_up, 4 * e + q - 1)
                cols = slice(c * HALF, (c + 1) * HALF)
                for w in range(2):
                    m = product(ps_gu[q % 2][w][:, :],
                                [(gu_h[r][:, k, w, :], gu_l[r][:, k, w, :], xT_h[:, k, cols], xT_l[:, k, cols])
                                 for k in range(KM)])
                m.then_inc(pe_gu, 1)

            def down(e, c):
                if c == 0:
                    pe.wait_ge(pool_dn, e + 1)
                last_half = halves_first(e) and e and c
                if not last_half:
                    pe.wait_ge(pool_act, 4 * e + (2 * c + 2 if halves_first(e) else c + 3))
                for w in range(2):
                    if last_half:
                        pe.wait_ge(pool_act, LAST + w + 1)
                    pe.wait_ge(dve_moe, 4 * e + 2 * c + w + 1)
                    for s in range(2):
                        t = 4 * c + 2 * w + s
                        cols = slice(t * P, (t + 1) * P)
                        m = product(ps_dn[c][w][:, s * M:(s + 1) * M],
                                    [(actT_h[:, r, cols], actT_l[:, r, cols], dn_h[:, r, :], dn_l[:, r, :]) for r in range(2)])
                    m.then_inc(pe_dn, 1)

            def expert(e):
                for q in range(4):
                    gate_up(e, q, True)
                    if q in (1, 2):
                        down(e - 1, q - 1)

            pe.wait_ge(dve_small, 2)
            turn_rows("b", 0, 4)
            turn_rows("b", 1, 5)
            pe.wait_ge(pool_gu[0], 1)
            for b in range(2):
                pe.wait_ge(dve_xT, 5 + b)
                cols = slice(b * T, (b + 1) * T)
                for w in range(2):
                    m = product(ps_gu[0][w][:, cols], [(gu_h[0][:, k, w, :], gu_l[0][:, k, w, :], xT_h[:, k, cols], xT_l[:, k, cols])
                                                       for k in range(KM)])
            m.then_inc(pe_gu, 1)
            turn_rows("b", 2, 6)
            cols = slice(0, HALF)
            pe.wait_ge(pool_gu[1], 1)
            for w in range(2):
                m = product(ps_gu[1][w][:, :], [(gu_h[1][:, k, w, :], gu_l[1][:, k, w, :], xT_h[:, k, cols], xT_l[:, k, cols])
                                                for k in range(KM)])
                if w == 0:
                    turn_rows("b", 3, 7)
            m.then_inc(pe_gu, 1)
            for c in range(2):
                if c:
                    pe.wait_ge(dve_xT, 8)
                cols = slice(c * HALF, (c + 1) * HALF)
                product(bank[6 + c][0:E, :], [(rwT_h[:, k, :], rwT_l[:, k, :], xT_h[:, k, cols], xT_l[:, k, cols])
                                              for k in range(KM)]).then_inc(pe_logitsT, 1)
            gate_up(0, 2, True)
            pe.wait_ge(act_logits, 2)
            for t in range(TILES):
                m = pe.transpose(bank[6][:, t * E:(t + 1) * E], logitsT[:, t * P:(t + 1) * P], ident[0:E, 0:E])
            m.then_inc(pe_logits, 1)
            gate_up(0, 3, True)
            gate_up(1, 0, True)
            pe.wait_ge(dve_route, 1)
            for t in range(TILES):
                m = pe.transpose(bank[4 + t // 4][0:E, (t % 4) * P:(t % 4 + 1) * P], route[:, t, :], ident[:, :])
                if t % 4 == 3:
                    m.then_inc(pe_routeT, 1)
            gate_up(1, 1, True)
            pe.wait_ge(dve_routeT, 2)
            for t in range(TILES):
                m = pe.matmul(bank[4 + t // 2][:, (t % 2) * M:(t % 2 + 1) * M], routeT[:, t * P:(t + 1) * P], dnb[:, :],
                              start=True, stop=True)
                if t % 2 == 1:
                    m.then_inc(pe_dnb, 1)
            down(0, 0)
            gate_up(1, 2, True)
            down(0, 1)
            gate_up(1, 3, True)
            with pe.Fori(2, E - 1) as e:
                expert(e)
            for q in range(4):
                gate_up(E - 1, q, True)
                if q < 2:
                    down(E - 2, q)
            down(E - 1, 0)
            down(E - 1, 1)


_INS = ["L0_attn_x", "L0_attn_wq", "L0_attn_wk", "L0_attn_wv", "L0_attn_wo", "L0_ffn_router_weight", "L0_ffn_router_bias",
        "L0_ffn_gate_up_proj", "L0_ffn_gate_up_proj_bias", "L0_ffn_down_proj", "L0_ffn_down_proj_bias"]


def _tables():
    half = D // 2
    freqs = np.power(np.float32(10000.0), -np.arange(half, dtype=np.float32) / np.float32(half)).astype(np.float32)
    rad = (freqs[:, None] * np.arange(T, dtype=np.float32)[None, :]).astype(np.float32)
    cos, sin = np.cos(rad).astype(np.float32), np.sin(rad).astype(np.float32)
    mask = np.zeros((P, T), np.float32)
    mask[:, P:] = np.where(np.arange(P)[None, :] > np.arange(P)[:, None], np.float32(NEG), np.float32(0.0))
    return {
        "rope_cos": np.concatenate([cos, cos], 0),
        "rope_sin": np.concatenate([-sin, sin], 0),
        "causal_mask": mask,
        "identity": np.eye(P, dtype=np.float32),
    }


def kernel(**inputs):
    import concourse.bacc as bacc
    from concourse.bass_utils import run_bass_kernel_spmd

    nc = bacc.Bacc("TRN2", target_bir_lowering=False, num_devices=1)
    arrays, args = {}, []
    given = {name: np.ascontiguousarray(inputs[name]) for name in _INS}
    for name, a in {**given, **_tables()}.items():
        arrays[f"in_{name}_dram"] = a
        args.append(nc.dram_tensor(f"in_{name}_dram", a.shape, mybir.dt.from_np(a.dtype), kind="ExternalInput").ap())
    args.append(nc.dram_tensor("out_0_dram", (B, T, M), F32, kind="ExternalOutput").ap())
    block_kernel(nc, *args)
    r = run_bass_kernel_spmd(nc, [arrays], core_ids=[0])
    return r.results[0]["out_0_dram"]
```
